# Optimizing a Trainium2 kernel written in Bass

```python
import numpy as np
import jax
import jax.numpy as jnp

def _softmax(x, axis=-1):
    return jax.nn.softmax(x, axis=axis)

def _gelu(x):
    return jax.nn.gelu(x, approximate=True)

def _silu(x):
    return jax.nn.silu(x)

def _sigmoid(x):
    return jax.nn.sigmoid(x)

def _layernorm(x, axis=-1, eps=1e-05):
    m = jnp.mean(x, axis=axis, keepdims=True)
    v = jnp.var(x, axis=axis, keepdims=True)
    return (x - m) / jnp.sqrt(v + eps)

def _scatter_add(tgt, idx, src, axis=0):
    return tgt.at[idx].add(src)

def _segment_sum(src, seg, n):
    return jax.ops.segment_sum(src, seg, n)
kernel_name = 'mk_metaformer_d2_conv_nchw128_r2_ecfd1e'

def setup_inputs(seed: int=0):
    np.random.seed(seed)
    _w = jnp.asarray

    def _rec_inputs():
        import jax
        import jax.numpy as jnp
        _gk = jax.random.key(seed)
        x = -4.117e-05 + 1 * jax.random.normal(jax.random.fold_in(_gk, 1), (2, 64, 256, 256), jnp.float32)
        return x
    x = _rec_inputs()

    def _L0_conv_setup():
        import jax, jax.numpy as jnp
        import numpy as np
        N_CLASSES = 64
        KSIZE = 3
        STRIDE = 1
        PAD = 1

        def _make_shift_kernel() -> jnp.ndarray:
            kernel = np.zeros((N_CLASSES, 1, KSIZE, KSIZE), dtype=np.float32)
            hks = KSIZE // 2
            ksq = KSIZE * KSIZE
            ch = 0
            for i in range(KSIZE):
                for j in range(KSIZE):
                    if i == hks and j == hks:
                        num_ch = N_CLASSES // ksq + N_CLASSES % ksq
                    else:
                        num_ch = N_CLASSES // ksq
                    kernel[ch:ch + num_ch, 0, i, j] = 1.0
                    ch += num_ch
            return jnp.asarray(kernel)
        key = jax.random.key(seed)
        x = jax.random.normal(key, (4, N_CLASSES, 256, 256), dtype=jnp.float32)
        kernel = _make_shift_kernel()
        return {'x': x, 'kernel': kernel}
    _L0_conv_all = _L0_conv_setup()
    _L0_conv_in = {k: v for k, v in _L0_conv_all.items() if k in ('kernel',)}
    del _L0_conv_all

    def _L0_ffn_setup():
        import jax, jax.numpy as jnp
        import numpy as np
        BN_EPS = 1e-05
        key = jax.random.key(seed)
        k1, k2, k3 = jax.random.split(key, 3)
        B, T, I, H = (32, 1024, 64, 64)
        x = jax.random.normal(k1, (B, T, I), dtype=jnp.float32)
        W = jax.random.normal(k2, (H, I), dtype=jnp.float32) * (1.0 / np.sqrt(I))
        V = jnp.linalg.qr(jax.random.normal(k3, (H, H), dtype=jnp.float32))[0]
        gamma = jnp.ones((H,), dtype=jnp.float32)
        beta = jnp.zeros((H,), dtype=jnp.float32)
        return {'x': x, 'W': W, 'V': V, 'gamma': gamma, 'beta': beta}
    _L0_ffn_all = _L0_ffn_setup()
    _L0_ffn_in = {k: v for k, v in _L0_ffn_all.items() if k in ('W', 'V', 'gamma', 'beta')}
    del _L0_ffn_all

    def _L1_conv_setup():
        import jax, jax.numpy as jnp
        import numpy as np
        DIM = 64
        HEADS = 8
        HDIM = DIM // HEADS
        KS = 4
        START = KS // 2
        EPS = 1e-06

        def _to_seq(t, head=HEADS, d=HDIM):
            b, c, h, w = t.shape
            return t.reshape(b, head, d, h * w).transpose(0, 3, 1, 2)

        def _feature_map(t):
            return jax.nn.elu(t) + 1.0
        key = jax.random.key(seed)
        ks = jax.random.split(key, 7)
        B, H, W = (4, 128, 128)
        x = jax.random.normal(ks[0], (B, DIM, H, W), dtype=jnp.float32)
        s = 0.05
        q_w = jax.random.normal(ks[1], (DIM, DIM), dtype=jnp.float32) * s
        q_b = jax.random.normal(ks[2], (DIM,), dtype=jnp.float32) * s
        kv_w = jax.random.normal(ks[3], (2 * DIM, DIM), dtype=jnp.float32) * s
        kv_b = jax.random.normal(ks[4], (2 * DIM,), dtype=jnp.float32) * s
        proj_w = jax.random.normal(ks[5], (DIM, DIM), dtype=jnp.float32) * s
        proj_b = jax.random.normal(ks[6], (DIM,), dtype=jnp.float32) * s
        return {'x': x, 'q_w': q_w, 'q_b': q_b, 'kv_w': kv_w, 'kv_b': kv_b, 'proj_w': proj_w, 'proj_b': proj_b}
    _L1_conv_all = _L1_conv_setup()
    _L1_conv_in = {k: v for k, v in _L1_conv_all.items() if k in ('q_w', 'q_b', 'kv_w', 'kv_b', 'proj_w', 'proj_b')}
    del _L1_conv_all

    def _L1_ffn_setup():
        import jax, jax.numpy as jnp
        import numpy as np
        B, S, D, E, H, O, K = (256, 1024, 64, 32, 256, 64, 8)
        key = jax.random.key(seed)
        k0, k1, k2, k3 = jax.random.split(key, 4)
        x = jax.random.normal(k0, (B, S, D), dtype=jnp.float32)
        gate_w = jax.random.normal(k1, (E, D), dtype=jnp.float32) * (1.0 / np.sqrt(D))
        gate_b = jnp.zeros((E,), dtype=jnp.float32)
        weight1 = jax.random.uniform(k2, (E, D + 1, H), dtype=jnp.float32, minval=-1.0, maxval=1.0) * (1.0 / np.sqrt(D + 1))
        weight2 = jax.random.uniform(k3, (E, H + 1, O), dtype=jnp.float32, minval=-1.0, maxval=1.0) * (1.0 / np.sqrt(H + 1))
        return {'x': x, 'gate_w': gate_w, 'gate_b': gate_b, 'weight1': weight1, 'weight2': weight2}
    _L1_ffn_all = _L1_ffn_setup()
    _L1_ffn_in = {k: v for k, v in _L1_ffn_all.items() if k in ('gate_w', 'gate_b', 'weight1', 'weight2')}
    del _L1_ffn_all
    return {'x': x, 'L0_conv_kernel': _L0_conv_in['kernel'], 'L0_ffn_W': _L0_ffn_in['W'], 'L0_ffn_V': _L0_ffn_in['V'], 'L0_ffn_gamma': _L0_ffn_in['gamma'], 'L0_ffn_beta': _L0_ffn_in['beta'], 'L1_conv_q_w': _L1_conv_in['q_w'], 'L1_conv_q_b': _L1_conv_in['q_b'], 'L1_conv_kv_w': _L1_conv_in['kv_w'], 'L1_conv_kv_b': _L1_conv_in['kv_b'], 'L1_conv_proj_w': _L1_conv_in['proj_w'], 'L1_conv_proj_b': _L1_conv_in['proj_b'], 'L1_ffn_gate_w': _L1_ffn_in['gate_w'], 'L1_ffn_gate_b': _L1_ffn_in['gate_b'], 'L1_ffn_weight1': _L1_ffn_in['weight1'], 'L1_ffn_weight2': _L1_ffn_in['weight2']}

def reference(x, L0_conv_kernel, L0_ffn_W, L0_ffn_V, L0_ffn_gamma, L0_ffn_beta, L1_conv_q_w, L1_conv_q_b, L1_conv_kv_w, L1_conv_kv_b, L1_conv_proj_w, L1_conv_proj_b, L1_ffn_gate_w, L1_ffn_gate_b, L1_ffn_weight1, L1_ffn_weight2):
    import jax
    import jax.numpy as jnp

    def _L0_conv_ref(x, kernel):
        import jax, jax.numpy as jnp
        import numpy as np
        N_CLASSES = 64
        KSIZE = 3
        STRIDE = 1
        PAD = 1

        def _make_shift_kernel() -> jnp.ndarray:
            kernel = np.zeros((N_CLASSES, 1, KSIZE, KSIZE), dtype=np.float32)
            hks = KSIZE // 2
            ksq = KSIZE * KSIZE
            ch = 0
            for i in range(KSIZE):
                for j in range(KSIZE):
                    if i == hks and j == hks:
                        num_ch = N_CLASSES // ksq + N_CLASSES % ksq
                    else:
                        num_ch = N_CLASSES // ksq
                    kernel[ch:ch + num_ch, 0, i, j] = 1.0
                    ch += num_ch
            return jnp.asarray(kernel)
        return jax.lax.conv_general_dilated(x, kernel, window_strides=(STRIDE, STRIDE), padding=[(PAD, PAD), (PAD, PAD)], dimension_numbers=('NCHW', 'OIHW', 'NCHW'), feature_group_count=N_CLASSES)

    def _L0_ffn_ref(x, W, V, gamma, beta):
        import jax, jax.numpy as jnp
        import numpy as np
        BN_EPS = 1e-05
        B, T, H = (x.shape[0], x.shape[1], W.shape[0])
        Wx = jnp.einsum('bti,hi->bth', x, W)
        flat = Wx.reshape(B * T, H)
        mean = jnp.mean(flat, axis=0)
        var = jnp.var(flat, axis=0)
        Wx = ((flat - mean) * jax.lax.rsqrt(var + BN_EPS) * gamma + beta).reshape(B, T, H)
        Vt = V.T

        def step(yt, wx_t):
            yt = jax.nn.sigmoid(wx_t + yt @ Vt)
            return (yt, yt)
        y0 = jnp.zeros((B, H), dtype=Wx.dtype)
        _, ys = jax.lax.scan(step, y0, jnp.swapaxes(Wx, 0, 1))
        return jnp.swapaxes(ys, 0, 1)

    def _L1_conv_ref(x, q_w, q_b, kv_w, kv_b, proj_w, proj_b):
        import jax, jax.numpy as jnp
        import numpy as np
        DIM = 64
        HEADS = 8
        HDIM = DIM // HEADS
        KS = 4
        START = KS // 2
        EPS = 1e-06

        def _to_seq(t, head=HEADS, d=HDIM):
            b, c, h, w = t.shape
            return t.reshape(b, head, d, h * w).transpose(0, 3, 1, 2)

        def _feature_map(t):
            return jax.nn.elu(t) + 1.0
        b, c, h, w = x.shape
        q = jnp.einsum('oc,bchw->bohw', q_w, x) + q_b[None, :, None, None]
        xs = x[:, :, START::KS, START::KS]
        kv = jnp.einsum('oc,bchw->bohw', kv_w, xs) + kv_b[None, :, None, None]
        k, v = (kv[:, :DIM], kv[:, DIM:])
        Q = _feature_map(_to_seq(q))
        K = _feature_map(_to_seq(k))
        V = _to_seq(v)
        S = V.shape[1]
        Vn = V / S
        KV = jnp.einsum('nshd,nshv->nhdv', K, Vn)
        Z = 1.0 / (jnp.einsum('nlhd,nhd->nlh', Q, K.sum(axis=1)) + EPS)
        out = jnp.einsum('nlhd,nhdv,nlh->nlhv', Q, KV, Z) * S
        out = out.transpose(0, 2, 3, 1).reshape(b, DIM, h, w)
        out = jnp.einsum('oc,bchw->bohw', proj_w, out) + proj_b[None, :, None, None]
        return out

    def _L1_ffn_ref(x, gate_w, gate_b, weight1, weight2):
        import jax, jax.numpy as jnp
        import numpy as np
        B, S, D, E, H, O, K = (256, 1024, 64, 32, 256, 64, 8)
        Bn, Sn, Dn = x.shape
        logits = jnp.einsum('bsd,ed->bse', x, gate_w) + gate_b
        probs = jax.nn.softmax(logits, axis=1)
        vals, idx = jax.lax.top_k(probs.transpose(0, 2, 1), K)
        topv = vals.transpose(0, 2, 1)
        topi = idx.transpose(0, 2, 1)
        flat_idx = topi.reshape(Bn, K * E)
        gathered = jnp.take_along_axis(x, flat_idx[:, :, None], axis=1)
        gathered = gathered.reshape(Bn, K, E, Dn)
        pooled = jnp.einsum('bked,bke->bed', gathered, topv)
        ones = jnp.ones((E, Bn, 1), dtype=x.dtype)
        h = jnp.concatenate([pooled.transpose(1, 0, 2), ones], axis=-1)
        h = jax.nn.gelu(jnp.einsum('ebd,edh->ebh', h, weight1), approximate=False)
        h = jnp.concatenate([h, ones], axis=-1)
        out = jnp.einsum('ebh,eho->ebo', h, weight2)
        out = out.transpose(1, 0, 2)
        weighted = jnp.einsum('beo,bke->bkeo', out, topv).reshape(Bn, K * E, O)
        outputs = jnp.zeros((Bn, Sn, O), dtype=x.dtype)
        outputs = outputs.at[jnp.arange(Bn)[:, None], flat_idx].add(weighted)
        return outputs

    def _gn(v, G=32, eps=1e-05):
        B_, C_, H_, W_ = v.shape
        g = v.reshape(B_, G, C_ // G, H_, W_)
        m = jnp.mean(g, axis=(2, 3, 4), keepdims=True)
        s = jnp.var(g, axis=(2, 3, 4), keepdims=True)
        return ((g - m) / jnp.sqrt(s + eps)).reshape(v.shape)

    def _ln_c(v, eps=1e-06):
        m = jnp.mean(v, axis=1, keepdims=True)
        s = jnp.var(v, axis=1, keepdims=True)
        return (v - m) / jnp.sqrt(s + eps)

    def _ln_t(v, eps=1e-05):
        m = jnp.mean(v, axis=-1, keepdims=True)
        s = jnp.var(v, axis=-1, keepdims=True)
        return (v - m) / jnp.sqrt(s + eps)

    def _to_tokens(v):
        B_, C_, H_, W_ = v.shape
        return v.reshape(B_, C_, H_ * W_).transpose(0, 2, 1)

    def _from_tokens(t, like):
        B_, C_, H_, W_ = like.shape
        return t.transpose(0, 2, 1).reshape(B_, C_, H_, W_)
    x = x + _L0_conv_ref(_ln_c(x), L0_conv_kernel)
    t = _to_tokens(x)
    t = t + _L0_ffn_ref(_ln_t(t), L0_ffn_W, L0_ffn_V, L0_ffn_gamma, L0_ffn_beta)
    x = _from_tokens(t, x)
    x = x + _L1_conv_ref(_ln_c(x), L1_conv_q_w, L1_conv_q_b, L1_conv_kv_w, L1_conv_kv_b, L1_conv_proj_w, L1_conv_proj_b)
    t = _to_tokens(x)
    t = t + _L1_ffn_ref(_ln_t(t), L1_ffn_gate_w, L1_ffn_gate_b, L1_ffn_weight1, L1_ffn_weight2)
    x = _from_tokens(t, x)
    return x

_drawn_inputs = setup_inputs


def setup_inputs(seed=0):
    import zlib

    import numpy as np

    out = dict(_drawn_inputs(seed))
    spreads = {'L0_ffn_gamma': (1.0, 0.6), 'L0_ffn_beta': (0.0, 0.585), 'L1_ffn_gate_b': (0.0, 0.1)}
    factors = {'L1_conv_q_w': 8.0,
     'L1_conv_q_b': 8.0,
     'L1_conv_kv_w': 8.0,
     'L1_conv_kv_b': 4.494,
     'L1_conv_proj_w': 3.79,
     'L1_ffn_gate_w': 8.0,
     'L1_ffn_weight1': 8.0,
     'L1_ffn_weight2': 8.0}
    for name, (base, spread) in spreads.items():
        noise = np.random.default_rng([zlib.crc32(name.encode()), seed]).standard_normal(out[name].shape)
        drawn = base * np.exp(spread * noise) if base else spread * noise
        out[name] = jnp.asarray(drawn.astype(out[name].dtype))
    for name, factor in factors.items():
        out[name] = (out[name] * factor).astype(out[name].dtype)
    return out
```

```python
from contextlib import ExitStack

import numpy as np

import concourse.bass as bass
from concourse import mybir

F32 = mybir.dt.float32
I32 = mybir.dt.int32
U32 = mybir.dt.uint32
ALU = mybir.AluOpType
ACT = mybir.ActivationFunctionType
AX = mybir.AxisListType

B, C, H, W = 2, 64, 256, 256
P = B * C
N = H * W
TILE = 512
BLOCK = 2048
TPB = BLOCK // TILE
NBLK = N // BLOCK
NT = N // TILE
ROWS = BLOCK // W
RPT = TILE // W
UNROLL = 4
HEADS, HD = 8, 8
EPS_C, EPS_T, EPS_BN, EPS_Z = 1e-6, 1e-5, 1e-5, 1e-6
E, K, HID = 32, 8, 256
SUB, SUB0 = 4, 2
NSUB = (H // SUB) * (W // SUB)
SUBB = NSUB // NBLK

REGIONS = 4
RLEN = N // REGIONS
CHUNKS = 512
CLEN = RLEN // CHUNKS
WARM = 12
STEPS = WARM + CLEN
RBLK = RLEN // BLOCK
STATE_TOL = 5e-7

CONST_NAMES = ["ident", "mean", "center", "heads", "pair"]


def constants():
    eye = np.eye(P)
    same_batch = np.kron(np.eye(B), np.ones((C, C)))
    mean = same_batch / C
    heads = np.kron(np.eye(B * HEADS), np.ones((HD, HD)))
    pair = np.kron(np.ones((B, B)), np.eye(C)) / B
    base = np.zeros((P, NBLK * K))
    for blk in range(NBLK):
        base[:64, blk * K:(blk + 1) * K] = blk * BLOCK
        base[64:, blk * K:(blk + 1) * K] = blk * BLOCK + TILE
    iota = np.tile(np.arange(2 * NBLK * K), (P, 1))
    slot = np.arange(E * K)
    later = [slot[None] > half * P + np.arange(P)[:, None] for half in range(2)]
    start = np.arange(P)[:, None] * N
    return np.concatenate([eye, mean, eye - mean, heads, pair, base, iota] + later + [start], 1).astype(np.float32)


def build_program(nc, x, conv_k, ffn_w, ffn_v, gamma, beta, q_w, q_b, kv_w, kv_b, proj_w, proj_b,
                  gate_w, gate_b, w1, w2, const, out, debug=None):
    stack = ExitStack()
    with stack:
        def sb(name, shape, dt=F32, where=stack):
            return where.enter_context(nc.sbuf_tensor(name, shape, dt))

        def sem(name, where):
            return where.enter_context(nc.semaphore(name))

        def dram(name, shape, dt=F32):
            return nc.dram_tensor(name, shape, dt, kind="Internal").ap()

        held = sem("held", stack)

        x1_d = dram("x1_scratch", (NBLK, P, BLOCK))
        xl_d = dram("xl_scratch", (NBLK, P, BLOCK))
        x2_d = dram("x2_scratch", (NBLK, P, BLOCK))
        tok_d = dram("token_scratch", (B * E * K,), I32)
        tokf_d = dram("token_f_scratch", (B * E * K,))
        prob_d = dram("prob_scratch", (B * E * K,))
        xt_d = dram("x3_transposed", (NBLK, P, BLOCK))
        x_v = x.rearrange("b c h w -> (b c) (h w)")
        out_v = out.rearrange("b c h w -> (b c) (h w)")

        cst = sb("cst", list(const.shape))
        ident, meanm, center, headm, pairm = (cst[:, i * P:(i + 1) * P] for i in range(5))
        base_c = cst[:, 5 * P:5 * P + NBLK * K]
        iota_c = cst[:, 5 * P + NBLK * K:5 * P + 3 * NBLK * K]
        later = cst[:, 5 * P + 3 * NBLK * K:5 * P + 3 * NBLK * K + 2 * E * K].rearrange("p (j s) -> p j s", j=2)
        start_c = cst[:, 5 * P + 3 * NBLK * K + 2 * E * K:]
        wT = sb("wT", [P, P])
        vT = sb("vT", [P, P])
        qT = sb("qT", [P, P])
        pT = sb("pT", [P, P])
        w_rows = sb("w_rows", [P, P])
        gT = sb("gT", [P, 2 * P])
        kvT = sb("kvT", [P, 2 * P])
        kvb = sb("kvb", [P, 2 * P])
        kk = sb("kk", [P, 9])
        cols = sb("cols", [P, 8])
        qb, pb, gb, gam, bet, eps_c, eps_t, eps_z = (cols[:, i:i + 1] for i in range(8))
        taps = sb("taps", [P, P])
        stats = sb("stats", [P, NT, 6])
        bn = sb("bn", [P, 8])
        ones = sb("ones", [P, 1])
        dT = sb("dT", [P, P])
        mT = sb("mT", [P, P])

        PE_TAPS = [4]
        ACT_TAPS = [0, 2, 8]
        DVE_TAPS = [1, 3, 5, 6, 7]

        with ExitStack() as ph:
            src = {n: sb(f"src_{n}", [P, P], F32, ph) for n in ("v", "q", "p", "g", "kv0", "kv1")}
            tp = [ph.enter_context(nc.psum_tensor(f"tp{i}", [P, P], F32)) for i in range(8)]
            zeroed, loaded, transposed, copied = (sem(n, ph) for n in ("zeroed", "loaded", "transposed", "copied"))
            blk = ph.enter_context(nc.Block())
            NLOAD = 1 + 2 * 5 + 2 + 2 * 5 + 4 + 2

            @blk.gpsimd
            def _(pool):
                for t in (w_rows, src["v"], src["q"], src["p"], src["g"], src["kv0"], src["kv1"]):
                    pool.memset(t[:, :], 0.0).then_inc(zeroed, 1)
                pool.memset(eps_c, EPS_C).then_inc(zeroed, 1)
                pool.memset(eps_t, EPS_T).then_inc(zeroed, 1)
                pool.memset(eps_z, EPS_Z).then_inc(zeroed, 1)
                pool.memset(ones[:, :], 1.0).then_inc(zeroed, 1)
                pool.memset(gT[:, :], 0.0).then_inc(zeroed, 1)

            @blk.sync
            def _(sp):
                sp.dma_start(cst[:, :], const).then_inc(loaded, 16)
                sp.wait_ge(zeroed, 7)
                for b in range(B):
                    d = slice(b * C, (b + 1) * C)
                    sp.dma_start(w_rows[d, d], ffn_w).then_inc(loaded, 16)
                    sp.dma_start(src["v"][d, d], ffn_v).then_inc(loaded, 16)
                    sp.dma_start(src["q"][d, d], q_w).then_inc(loaded, 16)
                    sp.dma_start(src["p"][d, d], proj_w).then_inc(loaded, 16)
                    sp.dma_start(src["g"][b * E:(b + 1) * E, d], gate_w).then_inc(loaded, 16)
                    sp.dma_start(src[f"kv{b}"][:, d], kv_w).then_inc(loaded, 16)
                    sp.dma_start(kk[d, :], conv_k.rearrange("c o i j -> c (o i j)")).then_inc(loaded, 16)
                    for col, vec in ((qb, q_b), (pb, proj_b), (gam, gamma), (bet, beta)):
                        sp.dma_start(col[d, :], vec.rearrange("(c o) -> c o", o=1)).then_inc(loaded, 16)
                    for part in range(2):
                        row = kv_b[part * C:(part + 1) * C].partition_broadcast(P)
                        sp.dma_start(kvb[:, part * P + b * C:part * P + (b + 1) * C], row).then_inc(loaded, 16)
                for r in range(4):
                    sp.dma_start(gb[r * E:(r + 1) * E, :], gate_b.rearrange("(c o) -> c o", o=1)).then_inc(loaded, 16)
                sp.wait_ge(loaded, 16 * (1 + 2 * 13 + 4))

            @blk.tensor
            def _(pe):
                pe.wait_ge(loaded, 16 * (1 + 2 * 13 + 4))
                order = (w_rows, src["v"], src["q"], src["p"], src["g"], src["kv0"], src["kv1"])
                for i, m in enumerate(order):
                    pe.transpose(tp[i][:, :], m[:, :], ident).then_inc(transposed, 1)

            @blk.vector
            def _(dve):
                dve.wait_ge(zeroed, 12)
                dve.wait_ge(transposed, 7)
                for i, t in enumerate((wT, vT, qT, pT)):
                    dve.tensor_copy(t[:, :], tp[i][:, :]).then_inc(copied, 1)
                dve.tensor_copy(gT[:, 0:64], tp[4][:, 0:64]).then_inc(copied, 1)
                dve.tensor_copy(gT[:, P + 64:2 * P], tp[4][:, 0:64]).then_inc(copied, 1)
                for b in range(B):
                    for part in range(2):
                        dve.tensor_copy(kvT[:, part * P + b * C:part * P + (b + 1) * C],
                                        tp[5 + b][:, part * C:(part + 1) * C]).then_inc(copied, 1)
                for i, t in enumerate(PE_TAPS):
                    dve.tensor_scalar(taps[:, i * P:(i + 1) * P], ident, kk[:, t:t + 1], None,
                                      ALU.mult).then_inc(copied, 1)

        regions = ExitStack()
        stack.enter_context(regions)
        XL = [sb("region0", [P, WARM + RLEN], F32, regions)]

        with ExitStack() as ph:
            PITCH = W + 2
            xin = sb("xin", [P, 4, BLOCK], F32, ph)
            xn = sb("xn", [P, 2, ROWS + 2, PITCH], F32, ph)
            x1 = sb("x1", [P, 2, BLOCK], F32, ph)
            xl = sb("xl", [P, 2, BLOCK], F32, ph)
            acc = sb("acc", [P, 2, RPT, W], F32, ph)
            sq = sb("sq", [P, 2, TILE], F32, ph)
            ln = sb("ln", [P, 2, TILE], F32, ph)
            rstd = sb("rstd", [P, 2, 2, TILE], F32, ph)
            prod = sb("tap_products", [P, len(ACT_TAPS), RPT, W], F32, ph)
            xr = sb("x_and_products", [P, TILE], F32, ph)
            psc = [[ph.enter_context(nc.psum_tensor(f"psc{l}{j}", [P, TILE], F32)) for j in range(2)] for l in range(2)]
            psv = [ph.enter_context(nc.psum_tensor(f"psv{l}", [P, TILE], F32)) for l in range(2)]
            pst = ph.enter_context(nc.psum_tensor("pst", [P, TILE], F32))
            psw = ph.enter_context(nc.psum_tensor("psw", [P, TILE], F32))
            S = lambda n: sem(n, ph)
            x_loaded = [S(f"x_loaded{r}") for r in range(4)]
            x1_stored = [S(f"x1_stored{r}") for r in range(2)]
            xl_stored = [S(f"xl_stored{r}") for r in range(2)]
            centered = [S("centered1"), S("centered2")]
            squared = [S("squared1"), S("squared2")]
            var_ready = [S("var_ready1"), S("var_ready2")]
            ln_done = [S("ln_done1"), S("ln_done2")]
            rstd_ready = [S("rstd_ready1"), S("rstd_ready2")]
            normed = [S("normed1"), S("normed2")]
            pads_ready = S("pads_ready")
            halo_ready = S("halo_ready")
            taps_ready = S("taps_ready")
            acc_step = S("acc_step")
            products = S("products")
            product_added = S("product_added")
            x1_ready = S("x1_ready")
            region0_loaded = S("region0_loaded")
            wx_ready = S("wx_ready")
            bn_done = S("bn_done")
            blk = ph.enter_context(nc.Block())
            NACC, NPROD = len(DVE_TAPS), len(ACT_TAPS)
            LAG = 3

            def schedule(eng, iteration):
                for u in range(UNROLL):
                    iteration(0, u)
                with eng.Fori(1, NBLK // UNROLL) as q:
                    for u in range(UNROLL):
                        iteration(q, u)
                for u in range(LAG):
                    iteration(NBLK // UNROLL, u)

            def stage(q, u, lag):
                k = 4 * q + (u - lag)
                active = not isinstance(k, int) or 0 <= k < NBLK
                return active, k, (u - lag) % 4

            def rounds(q, u, lag, ring):
                return (4 // ring) * q + (u - lag) // ring

            def tile_cols(s):
                return slice(s * TILE, (s + 1) * TILE)

            @blk.sync
            def _(sp):
                def load(q, u, lead):
                    on, k, r = stage(q, u, -lead)
                    if not on:
                        return
                    if not isinstance(k, int) or k >= 4:
                        sp.wait_ge(x1_ready, 4 * k - 12)
                    sp.dma_start(xin[:, r, :], x_v[:, bass.ds(k * BLOCK, BLOCK)]).then_inc(x_loaded[r], 16)

                def iteration(q, u):
                    load(q, u, 2)
                    on, k, r = stage(q, u, 1)
                    if on:
                        sp.wait_ge(x1_ready, 4 * k + 4)
                        sp.dma_start(x1_d[bass.ds(k, 1), :, :].rearrange("o p n -> p (o n)"),
                                     x1[:, r % 2, :]).then_inc(x1_stored[r % 2], 16)
                    on, k, r = stage(q, u, 2)
                    if on:
                        sp.wait_ge(normed[1], 4 * k + 4)
                        sp.dma_start(xl_d[bass.ds(k, 1), :, :].rearrange("o p n -> p (o n)"),
                                     xl[:, r % 2, :]).then_inc(xl_stored[r % 2], 16)

                load(0, 0, 0)
                load(0, 0, 1)
                last = NBLK // UNROLL - 1
                for u in range(UNROLL):
                    iteration(0, u)
                with sp.Fori(1, last) as q:
                    for u in range(UNROLL):
                        iteration(q, u)
                for j in range(RBLK):
                    if j < 2:
                        sp.wait_ge(xl_stored[j], 16 * RBLK)
                    sp.dma_start(XL[0][:, WARM + j * BLOCK:WARM + (j + 1) * BLOCK],
                                 xl_d[j, :, :]).then_inc(region0_loaded, 16)
                for u in range(UNROLL + LAG):
                    iteration(last, u)
                for r in range(2):
                    sp.wait_ge(x1_stored[r], 16 * NBLK // 2)
                    sp.wait_ge(xl_stored[r], 16 * NBLK // 2)
                sp.wait_ge(region0_loaded, 16 * RBLK)

            @blk.tensor
            def _(pe):
                def iteration(q, u):
                    for s in range(TPB):
                        on, k, r = stage(q, u, 0)
                        if on:
                            if s == 0:
                                pe.wait_ge(x_loaded[r], 16 * (rounds(q, u, 0, 4) + 1))
                            g = 4 * k + s
                            if not isinstance(g, int) or g >= 2:
                                pe.wait_ge(normed[0], g - 1)
                            pe.matmul(psc[0][s % 2][:, :], center, xin[:, r, tile_cols(s)],
                                      start=True, stop=True).then_inc(centered[0], 1)
                        on, k, r = stage(q, u, 1)
                        if on:
                            g = 4 * k + s
                            if s == 0:
                                pe.wait_ge(normed[0], 4 * k + 4)
                                pe.wait_ge(halo_ready, 1 if isinstance(k, int) and k == 0 else 2 * k)
                            if s == TPB - 1:
                                pe.wait_ge(halo_ready, 2 * k + 3)
                            if not isinstance(g, int) or g >= 1:
                                pe.wait_ge(acc_step, NACC * g - NACC + 1)
                            for n, t in enumerate(PE_TAPS):
                                i, j = t // 3, t % 3
                                m = pe.matmul(pst[:, :].rearrange("p (r w) -> p r w", w=W),
                                              taps[:, n * P:(n + 1) * P],
                                              xn[:, r % 2, RPT * s + i:RPT * s + i + RPT, j:j + W],
                                              start=(n == 0), stop=(n == len(PE_TAPS) - 1))
                            m.then_inc(taps_ready, 1)
                        on, k, r = stage(q, u, 0)
                        if on:
                            g = 4 * k + s
                            pe.wait_ge(squared[0], g + 1)
                            if not isinstance(g, int) or g >= 1:
                                pe.wait_ge(ln_done[0], g)
                            pe.matmul(psv[0][:, :], meanm, sq[:, 0, :], start=True,
                                      stop=True).then_inc(var_ready[0], 1)
                        on, k, r = stage(q, u, 2)
                        if on:
                            g = 4 * k + s
                            pe.wait_ge(x1_ready, g + 1)
                            if not isinstance(g, int) or g >= 2:
                                pe.wait_ge(normed[1], g - 1)
                            pe.matmul(psc[1][s % 2][:, :], center, x1[:, r % 2, tile_cols(s)],
                                      start=True, stop=True).then_inc(centered[1], 1)
                        on, k, r = stage(q, u, 3)
                        if on:
                            g = 4 * k + s
                            pe.wait_ge(normed[1], g + 1)
                            if not isinstance(g, int) or g >= 1:
                                pe.wait_ge(bn_done, g)
                            pe.matmul(psw[:, :], wT[:, :], xl[:, r % 2, tile_cols(s)],
                                      start=True, stop=True).then_inc(wx_ready, 1)
                        on, k, r = stage(q, u, 2)
                        if on:
                            g = 4 * k + s
                            pe.wait_ge(squared[1], g + 1)
                            if not isinstance(g, int) or g >= 1:
                                pe.wait_ge(ln_done[1], g)
                            pe.matmul(psv[1][:, :], meanm, sq[:, 1, :], start=True,
                                      stop=True).then_inc(var_ready[1], 1)
                schedule(pe, iteration)

            @blk.scalar
            def _(act):
                act.preload_act_table_set("natural_log_exp_and_others")

                def square(q, u, s, l):
                    on, k, _ = stage(q, u, 2 * l)
                    if not on:
                        return
                    g = 4 * k + s
                    act.wait_ge(centered[l], g + 1)
                    if not isinstance(g, int) or g >= 1:
                        act.wait_ge(var_ready[l], g)
                    act.activation(sq[:, l, :], psc[l][s % 2][:, :], ACT.Square).then_inc(squared[l], 1)

                def rsqrt(q, u, s, l):
                    on, k, _ = stage(q, u, 2 * l)
                    if not on:
                        return
                    g = 4 * k + s
                    act.wait_ge(var_ready[l], g + 1)
                    if not isinstance(g, int) or g >= 1:
                        act.wait_ge(rstd_ready[l], g)
                    act.activation(ln[:, l, :], psv[l][:, :], ACT.Ln,
                                   bias=(eps_c, eps_t)[l]).then_inc(ln_done[l], 1)
                    act.wait_ge(ln_done[l], g + 1)
                    if not isinstance(g, int) or g >= 2:
                        act.wait_ge(normed[l], g - 1)
                    act.activation(rstd[:, l, s % 2, :], ln[:, l, :], ACT.Exp,
                                   scale=-0.5).then_inc(rstd_ready[l], 1)

                def tap_product(q, u, s, n):
                    on, k, r = stage(q, u, 1)
                    if not on:
                        return
                    g = 4 * k + s
                    if n == 0 and s == 0:
                        act.wait_ge(normed[0], 4 * k + 4)
                        act.wait_ge(halo_ready, 1 if isinstance(k, int) and k == 0 else 2 * k)
                    if n == 0 and s == TPB - 1:
                        act.wait_ge(halo_ready, 2 * k + 3)
                    if not isinstance(g, int) or g >= 1:
                        act.wait_ge(product_added, NPROD * (g - 1) + n + 1)
                    i, j = ACT_TAPS[n] // 3, ACT_TAPS[n] % 3
                    act.activation(prod[:, n, :, :], xn[:, r % 2, RPT * s + i:RPT * s + i + RPT, j:j + W],
                                   ACT.Copy, scale=kk[:, ACT_TAPS[n]:ACT_TAPS[n] + 1]).then_inc(products, 1)

                def iteration(q, u):
                    for s in range(TPB):
                        square(q, u, s, 0)
                        tap_product(q, u, s, 0)
                        tap_product(q, u, s, 1)
                        rsqrt(q, u, s, 0)
                        square(q, u, s, 1)
                        tap_product(q, u, s, 2)
                        rsqrt(q, u, s, 1)
                schedule(act, iteration)

            @blk.gpsimd
            def _(pool):
                pool.memset(xn[:, :, :, :].rearrange("p a r w -> p (a r w)"), 0.0).then_inc(pads_ready, 1)
                pool.wait_ge(pads_ready, 1)
                pool.sem_inc(halo_ready, 1)

                def halos(q, u):
                    on, k, r = stage(q, u, 0)
                    first = isinstance(k, int) and k == 0
                    if on and not first:
                        pool.wait_ge(normed[0], 4 * k + 1)
                        pool.sem_inc(held, 1)
                        pool.tensor_copy(xn[:, (r + 1) % 2, ROWS + 1, 1:W + 1],
                                         xn[:, r % 2, 1, 1:W + 1]).then_inc(halo_ready, 1)
                    elif isinstance(k, int) and k == NBLK:
                        pool.memset(xn[:, (r + 1) % 2, ROWS + 1, 1:W + 1], 0.0).then_inc(halo_ready, 1)

                def last_row(q, u):
                    on, k, r = stage(q, u, 0)
                    if on:
                        pool.wait_ge(normed[0], 4 * k + 4)
                        pool.wait_ge(acc_step, NACC * 4 * k)
                        pool.sem_inc(held, 1)
                        pool.tensor_copy(xn[:, (r + 1) % 2, 0, 1:W + 1],
                                         xn[:, r % 2, ROWS, 1:W + 1]).then_inc(halo_ready, 1)

                def iteration(q, u):
                    halos(q, u)
                    on, k, r = stage(q, u, 1)
                    if on:
                        for s in range(TPB):
                            g = 4 * k + s
                            if not isinstance(g, int) or g >= 1:
                                pool.wait_ge(x1_ready, g)
                            for n in range(NPROD):
                                pool.wait_ge(products, NPROD * g + n + 1)
                                if n:
                                    pool.wait_ge(product_added, NPROD * g + n)
                                pool.tensor_tensor(xr[:, :], prod[:, n, :, :].rearrange("p r w -> p (r w)"),
                                                   xr[:, :] if n else xin[:, r, tile_cols(s)],
                                                   ALU.add).then_inc(product_added, 1)
                            pool.wait_ge(product_added, NPROD * g + NPROD)
                            pool.wait_ge(acc_step, NACC * g + NACC)
                            if s == 0 and (not isinstance(k, int) or k >= 2):
                                pool.wait_ge(centered[1], 4 * k - 4)
                                pool.wait_ge(x1_stored[r % 2], 16 * rounds(q, u, 1, 2))
                            pool.tensor_tensor(x1[:, r % 2, tile_cols(s)],
                                               acc[:, s % 2, :, :].rearrange("p r w -> p (r w)"),
                                               xr[:, :], ALU.add).then_inc(x1_ready, 1)
                    last_row(q, u)
                schedule(pool, iteration)

            @blk.vector
            def _(dve):
                dve.wait_ge(pads_ready, 1)

                def iteration(q, u):
                    for s in range(TPB):
                        on, k, r = stage(q, u, 0)
                        if on:
                            g = 4 * k + s
                            if s == 0 and (not isinstance(k, int) or k >= 2):
                                dve.wait_ge(x1_ready, 4 * k - 4)
                                dve.wait_ge(halo_ready, 2 * k)
                            dve.wait_ge(rstd_ready[0], g + 1)
                            dve.tensor_tensor(xn[:, r % 2, 1 + RPT * s:1 + RPT * (s + 1), 1:W + 1],
                                              psc[0][s % 2][:, :].rearrange("p (r w) -> p r w", w=W),
                                              rstd[:, 0, s % 2, :].rearrange("p (r w) -> p r w", w=W),
                                              ALU.mult).then_inc(normed[0], 1)
                        on, k, r = stage(q, u, 1)
                        if on:
                            g = 4 * k + s
                            if s == 0:
                                dve.wait_ge(normed[0], 4 * k + 4)
                                dve.wait_ge(halo_ready, 1 if isinstance(k, int) and k == 0 else 2 * k)
                            if s == TPB - 1:
                                dve.wait_ge(halo_ready, 2 * k + 3)
                            dve.wait_ge(taps_ready, g + 1)
                            if not isinstance(g, int) or g >= 2:
                                dve.wait_ge(x1_ready, g - 1)
                            for n, t in enumerate(DVE_TAPS):
                                i, j = t // 3, t % 3
                                if n:
                                    dve.wait_ge(acc_step, NACC * g + n)
                                    prev = acc[:, s % 2, :, :]
                                else:
                                    prev = pst[:, :].rearrange("p (r w) -> p r w", w=W)
                                dve.scalar_tensor_tensor(
                                    out=acc[:, s % 2, :, :],
                                    in0=xn[:, r % 2, RPT * s + i:RPT * s + i + RPT, j:j + W],
                                    scalar=kk[:, t:t + 1], in1=prev, op0=ALU.mult,
                                    op1=ALU.add).then_inc(acc_step, 1)
                        on, k, r = stage(q, u, 2)
                        if on:
                            g = 4 * k + s
                            if s == 0 and (not isinstance(k, int) or k >= 2):
                                dve.wait_ge(wx_ready, 4 * k - 4)
                                dve.wait_ge(xl_stored[r % 2], 16 * rounds(q, u, 2, 2))
                            dve.wait_ge(rstd_ready[1], g + 1)
                            dve.tensor_tensor(xl[:, r % 2, tile_cols(s)], psc[1][s % 2][:, :],
                                              rstd[:, 1, s % 2, :], ALU.mult).then_inc(normed[1], 1)
                        on, k, r = stage(q, u, 3)
                        if on:
                            g = 4 * k + s
                            dve.wait_ge(wx_ready, g + 1)
                            dve.bn_stats(stats[:, bass.ds(g, 1), :].rearrange("p o n -> p (o n)"),
                                         psw[:, :]).then_inc(bn_done, 1)
                schedule(dve, iteration)

        with ExitStack() as ph:
            wps = ph.enter_context(nc.psum_tensor("wps", [P, P], F32))
            bps = ph.enter_context(nc.psum_tensor("bps", [P, 2], F32))
            step, mm = sem("bn_step", ph), sem("bn_mm", ph)
            rs = sem("bn_rs", ph)
            blk = ph.enter_context(nc.Block())

            @blk.vector
            def _(dve):
                dve.bn_aggr(bn[:, 0:2], stats[:, :, :].rearrange("p t n -> p (t n)")).then_inc(step, 1)
                dve.wait_ge(mm, 1)
                dve.tensor_copy(bn[:, 2:3], bps[:, 0:1]).then_inc(step, 1)
                dve.wait_ge(step, 2)
                dve.tensor_tensor(bn[:, 3:4], bn[:, 0:1], bn[:, 2:3], ALU.subtract).then_inc(step, 1)
                dve.wait_ge(step, 3)
                dve.scalar_tensor_tensor(out=bn[:, 4:5], in0=bn[:, 3:4], scalar=bn[:, 3:4],
                                         in1=bn[:, 1:2], op0=ALU.mult, op1=ALU.add).then_inc(step, 1)
                dve.wait_ge(rs, 2)
                dve.tensor_tensor(bn[:, 6:7], bn[:, 3:4], gam, ALU.mult).then_inc(step, 1)
                dve.wait_ge(step, 5)
                dve.tensor_tensor(bn[:, 4:5], bn[:, 2:3], bn[:, 6:7], ALU.mult).then_inc(step, 1)
                dve.wait_ge(step, 6)
                dve.tensor_tensor(bn[:, 7:8], bet, bn[:, 4:5], ALU.subtract).then_inc(step, 1)
                dve.tensor_scalar(w_rows[:, :], w_rows[:, :], bn[:, 6:7], None, ALU.mult).then_inc(step, 1)
                dve.wait_ge(mm, 3)
                dve.tensor_copy(wT[:, :], wps[:, :]).then_inc(step, 1)

            @blk.tensor
            def _(pe):
                pe.wait_ge(step, 1)
                pe.matmul(bps[:, 0:1], pairm, bn[:, 0:1], start=True, stop=True).then_inc(mm, 1)
                pe.wait_ge(step, 4)
                pe.matmul(bps[:, 1:2], pairm, bn[:, 4:5], start=True, stop=True).then_inc(mm, 1)
                pe.wait_ge(step, 8)
                pe.transpose(wps[:, :], w_rows[:, :], ident).then_inc(mm, 1)

            @blk.scalar
            def _(act):
                act.preload_act_table_set("natural_log_exp_and_others")
                act.wait_ge(mm, 2)
                act.activation(bn[:, 5:6], bps[:, 1:2], ACT.Ln, bias=eps_t).then_inc(rs, 1)
                act.wait_ge(rs, 1)
                act.activation(bn[:, 3:4], bn[:, 5:6], ACT.Exp, scale=-0.5).then_inc(rs, 1)

        bias_w = bn[:, 7:8]
        keys = ExitStack()
        stack.enter_context(keys)
        xsub = sb("xsub", [P, NSUB], F32, keys)
        flag = sb("flag", [P, 1], I32, keys)

        def take_keys(pool, block, src_rows):
            v = src_rows.rearrange("p (r w) -> p r w", w=W)
            return pool.tensor_copy(
                xsub[:, bass.ds(block * SUBB, SUBB)].rearrange("p (r w) -> p r w", w=W // SUB),
                v[:, SUB0:ROWS:SUB, SUB0:W:SUB])

        with ExitStack() as ph:
            XL.append(sb("region1", [P, WARM + RLEN], F32, ph))
            ws = sb("warm_state", [P, 2, CHUNKS], F32, ph)
            reached = sb("reached", [P, CHUNKS], F32, ph)
            true = sb("true_state", [P, 1 + CHUNKS], F32, ph)
            diff = sb("diff", [P, CHUNKS], F32, ph)
            dmax = sb("dmax", [P, REGIONS + 1], F32, ph)
            dall = sb("dall", [1, P + 2], F32, ph)
            xb = sb("x1_block", [P, 3, BLOCK], F32, ph)
            pss = [ph.enter_context(nc.psum_tensor(f"pss{j}", [P, CHUNKS], F32)) for j in range(2)]
            pdm = ph.enter_context(nc.psum_tensor("pdm", [1, P], F32))
            S = lambda n: sem(n, ph)
            warm_loaded = [S(f"warm_loaded{j}") for j in range(2)]
            region_loaded = [S(f"region_loaded{j}") for j in range(2)]
            x1_loaded = [S(f"x1_loaded{j}") for j in range(3)]
            x2_stored = [S(f"x2_stored{j}") for j in range(3)]
            sums_ready, y_ready = S("sums_ready"), S("y_ready")
            fixed = S("fixed")
            kept = S("states_kept")
            added = S("added")
            key_taken = S("key_taken")
            checked = S("checked")
            dstep = S("dstep")
            dmm = S("dmm")
            zero_warm = S("zero_warm")
            blk = ph.enter_context(nc.Block())
            UN = 4
            last_warm = (WARM - 1) % 2

            def at(buf, n):
                return XL[buf][:, bass.ds(n, CHUNKS, step=CLEN)]

            @blk.sync
            def _(sp):
                def load_region(r):
                    b = r % 2
                    if r >= 2:
                        sp.wait_ge(added, RBLK * (r - 1))
                        sp.wait_ge(kept, 2 * (r - 1))
                    if r:
                        sp.dma_start(XL[b][:, 0:WARM],
                                     xl_d[r * RBLK - 1, :, BLOCK - WARM:BLOCK]).then_inc(warm_loaded[b], 16)
                    for j in range(RBLK):
                        sp.dma_start(XL[b][:, WARM + j * BLOCK:WARM + (j + 1) * BLOCK],
                                     xl_d[r * RBLK + j, :, :]).then_inc(region_loaded[b], 16)

                load_region(1)
                for r in range(REGIONS):
                    for j in range(RBLK):
                        k = r * RBLK + j
                        slot = k % 3
                        if k >= 3:
                            sp.wait_ge(x2_stored[slot], 16 * (k // 3))
                            sp.wait_ge(key_taken, k - 2)
                        sp.dma_start(xb[:, slot, :], x1_d[k, :, :]).then_inc(x1_loaded[slot], 16)
                        if k >= 1:
                            sp.wait_ge(added, k)
                            p = k - 1
                            sp.dma_start(x2_d[p, :, :], xb[:, p % 3, :]).then_inc(x2_stored[p % 3], 16)
                        if j == 0 and 1 <= r < REGIONS - 1:
                            load_region(r + 1)
                sp.wait_ge(added, NBLK)
                sp.dma_start(x2_d[NBLK - 1, :, :], xb[:, (NBLK - 1) % 3, :]).then_inc(x2_stored[(NBLK - 1) % 3], 16)
                for slot in range(3):
                    sp.wait_ge(x2_stored[slot], 16 * len(range(slot, NBLK, 3)))

            @blk.tensor
            def _(pe):
                def inject(b, n, par):
                    pe.matmul(pss[par][:, :], wT[:, :], at(b, n), start=True, stop=False)

                for r in range(REGIONS):
                    b, base = r % 2, r * STEPS
                    if r == 0:
                        pe.wait_ge(zero_warm, 1)
                    else:
                        pe.wait_ge(warm_loaded[b], 16 * ((r + 1) // 2))
                    if r:
                        pe.wait_ge(region_loaded[b], 16 * RBLK * ((r + 1) // 2))
                    if r:
                        pe.wait_ge(y_ready, base)
                    pe.matmul(pss[0][:, :], wT[:, :], at(b, 0), start=True, stop=True).then_inc(sums_ready, 1)
                    for n in range(1, WARM):
                        inject(b, n, n % 2)
                        pe.wait_ge(y_ready, base + n)
                        pe.matmul(pss[n % 2][:, :], vT[:, :], ws[:, (n - 1) % 2, :], start=False,
                                  stop=True).then_inc(sums_ready, 1)
                    inject(b, WARM, WARM % 2)
                    pe.wait_ge(y_ready, base + WARM)
                    if r == 0:
                        pe.wait_ge(fixed, 1)
                    pe.matmul(pss[WARM % 2][:, :], vT[:, :], ws[:, last_warm, :], start=False,
                              stop=True).then_inc(sums_ready, 1)

                    def step(n, par):
                        inject(b, n, par)
                        pe.wait_ge(y_ready, n + base)
                        pe.matmul(pss[par][:, :], vT[:, :], at(b, n - 1), start=False,
                                  stop=True).then_inc(sums_ready, 1)
                    for v in range(1, UN):
                        step(WARM + v, v % 2)
                    with pe.Fori(1, CLEN // UN) as t:
                        for v in range(UN):
                            step(t * UN + (WARM + v), v % 2)
                pe.wait_ge(checked, REGIONS)
                pe.transpose(pdm[0:1, :], dmax[:, REGIONS:REGIONS + 1], ident).then_inc(dmm, 1)

            @blk.scalar
            def _(act):
                act.preload_act_table(ACT.Sigmoid)
                for r in range(REGIONS):
                    b, base = r % 2, r * STEPS
                    for n in range(WARM):
                        act.wait_ge(sums_ready, base + n + 1)
                        if n == last_warm and r:
                            act.wait_ge(kept, 2 * r - 1)
                        act.activation(ws[:, n % 2, :], pss[n % 2][:, :], ACT.Sigmoid,
                                       bias=bias_w).then_inc(y_ready, 1)
                    if r == 0:
                        act.wait_ge(y_ready, WARM)
                        act.activation(ws[:, last_warm, 0:1], ws[:, last_warm, 0:1], ACT.Copy,
                                       scale=0.0).then_inc(fixed, 1)

                    with act.Fori(0, CLEN // UN) as t:
                        for v in range(UN):
                            act.wait_ge(sums_ready, t * UN + (base + WARM + v + 1))
                            act.activation(at(b, t * UN + (WARM + v)), pss[v % 2][:, :], ACT.Sigmoid,
                                           bias=bias_w).then_inc(y_ready, 1)

            @blk.gpsimd
            def _(pool):
                pool.memset(XL[0][:, 0:WARM], 0.0).then_inc(zero_warm, 1)
                pool.memset(true[:, 0:1], 0.0).then_inc(zero_warm, 1)
                for r in range(REGIONS):
                    b = r % 2
                    pool.wait_ge(y_ready, r * STEPS + WARM)
                    if r == 0:
                        pool.wait_ge(fixed, 1)
                    else:
                        pool.wait_ge(checked, r)
                    pool.tensor_copy(reached[:, :], ws[:, last_warm, :]).then_inc(kept, 1)
                    pool.wait_ge(y_ready, (r + 1) * STEPS)
                    pool.tensor_copy(true[:, 1:1 + CHUNKS],
                                     XL[b][:, WARM + CLEN - 1:WARM + RLEN:CLEN]).then_inc(kept, 1)
                    for j in range(RBLK):
                        k = r * RBLK + j
                        pool.wait_ge(added, k + 1)
                        take_keys(pool, k, xb[:, k % 3, :]).then_inc(key_taken, 1)

            @blk.vector
            def _(dve):
                n = 0
                dve.wait_ge(zero_warm, 2)
                for r in range(REGIONS):
                    dve.wait_ge(kept, 2 * r + 2)
                    dve.tensor_tensor(diff[:, :], reached[:, :], true[:, 0:CHUNKS],
                                      ALU.subtract).then_inc(dstep, 1)
                    n += 1
                    dve.wait_ge(dstep, n)
                    dve.tensor_reduce(dmax[:, r:r + 1], diff[:, :], AX.X, ALU.max,
                                      apply_absolute_value=True).then_inc(dstep, 1)
                    dve.tensor_copy(true[:, 0:1], true[:, CHUNKS:CHUNKS + 1]).then_inc(dstep, 1)
                    n += 2
                    dve.wait_ge(dstep, n)
                    if r == REGIONS - 1:
                        dve.tensor_reduce(dmax[:, REGIONS:REGIONS + 1], dmax[:, 0:REGIONS], AX.X,
                                          ALU.max).then_inc(checked, 1)
                    else:
                        dve.sem_inc(checked, 1)
                    dve.wait_ge(y_ready, (r + 1) * STEPS)
                    for j in range(RBLK):
                        k = r * RBLK + j
                        dve.wait_ge(x1_loaded[k % 3], 16 * (k // 3 + 1))
                        dve.tensor_tensor(xb[:, k % 3, :], xb[:, k % 3, :],
                                          XL[r % 2][:, WARM + j * BLOCK:WARM + (j + 1) * BLOCK],
                                          ALU.add).then_inc(added, 1)
                dve.wait_ge(dmm, 1)
                dve.tensor_copy(dall[0:1, 0:P], pdm[0:1, :]).then_inc(dstep, 1)
                dve.wait_ge(dstep, n + 1)
                dve.tensor_reduce(dall[0:1, P:P + 1], dall[0:1, 0:P], AX.X, ALU.max).then_inc(dstep, 1)
                dve.wait_ge(dstep, n + 2)
                dve.tensor_scalar(flag[0:1, :], dall[0:1, P:P + 1], STATE_TOL, None,
                                  ALU.is_le).then_inc(dstep, 1)

        with ExitStack() as ph:
            xs = sb("seq_xl", [P, BLOCK], F32, ph)
            ys = sb("seq_y", [P, 1 + BLOCK], F32, ph)
            xr = sb("seq_x", [P, BLOCK], F32, ph)
            pq = ph.enter_context(nc.psum_tensor("pq", [P, 1], F32))
            S = lambda n: sem(n, ph)
            seq_loaded, seq_sums, seq_y = S("seq_loaded"), S("seq_sums"), S("seq_y_ready")
            seq_added, seq_carried, seq_stored, seq_keys = S("seq_added"), S("seq_carried"), S("seq_stored"), S("seq_keys")
            blk = ph.enter_context(nc.Block())

            def unreached(eng):
                return eng.value_load(flag[0:1, 0:1], min_val=0, max_val=1) == 0

            @blk.sync
            def _(sp):
                with sp.If(unreached(sp)):
                    with sp.Fori(0, NBLK) as k:
                        sp.wait_ge(seq_added, k + 1)
                        sp.sem_inc(held, 1)
                        sp.wait_ge(seq_keys, k + 1)
                        sp.sem_inc(held, 1)
                        sp.wait_ge(seq_stored, k * 16 + 16)
                        sp.dma_start(xs[:, :], xl_d[bass.ds(k, 1), :, :].rearrange("o p n -> p (o n)")).then_inc(seq_loaded, 16)
                        sp.dma_start(xr[:, :], x1_d[bass.ds(k, 1), :, :].rearrange("o p n -> p (o n)")).then_inc(seq_loaded, 16)
                        sp.wait_ge(seq_added, k + 2)
                        sp.sem_inc(held, 1)
                        sp.dma_start(x2_d[bass.ds(k, 1), :, :].rearrange("o p n -> p (o n)"), xr[:, :]).then_inc(seq_stored, 16)
                    sp.wait_ge(seq_stored, 16 * NBLK + 16)

            @blk.tensor
            def _(pe):
                with pe.If(unreached(pe)):
                    with pe.Fori(0, NBLK) as k:
                        pe.wait_ge(seq_loaded, k * 32 + 32)
                        pe.wait_ge(seq_carried, k + 1)
                        pe.sem_inc(held, 1)
                        with pe.Fori(0, BLOCK) as t:
                            pe.wait_ge(seq_y, k * BLOCK + t + 1)
                            pe.matmul(pq[:, :], wT[:, :], xs[:, bass.ds(t, 1)], start=True, stop=False)
                            pe.matmul(pq[:, :], vT[:, :], ys[:, bass.ds(t, 1)], start=False,
                                      stop=True).then_inc(seq_sums, 1)

            @blk.scalar
            def _(act):
                act.preload_act_table(ACT.Sigmoid)
                with act.If(unreached(act)):
                    with act.Fori(0, NBLK) as k:
                        act.wait_ge(seq_added, k + 1)
                        act.wait_ge(seq_carried, k + 1)
                        with act.Fori(0, BLOCK) as t:
                            act.wait_ge(seq_sums, k * BLOCK + t + 1)
                            act.activation(ys[:, bass.ds(t + 1, 1)], pq[:, :], ACT.Sigmoid,
                                           bias=bias_w).then_inc(seq_y, 1)

            @blk.vector
            def _(dve):
                with dve.If(unreached(dve)):
                    for ahead, n in ((seq_y, 1), (seq_added, 1), (seq_keys, 1), (seq_stored, 16)):
                        dve.sem_inc(ahead, n)
                    dve.memset(ys[:, 0:1], 0.0).then_inc(seq_carried, 1)
                    with dve.Fori(0, NBLK) as k:
                        dve.wait_ge(seq_loaded, k * 32 + 32)
                        dve.wait_ge(seq_y, k * BLOCK + BLOCK + 1)
                        dve.tensor_tensor(xr[:, :], xr[:, :], ys[:, 1:1 + BLOCK], ALU.add).then_inc(seq_added, 1)
                        dve.tensor_copy(ys[:, 0:1], ys[:, BLOCK:BLOCK + 1]).then_inc(seq_carried, 1)

            @blk.gpsimd
            def _(pool):
                with pool.If(unreached(pool)):
                    with pool.Fori(0, NBLK) as k:
                        pool.wait_ge(seq_added, k + 2)
                        take_keys(pool, k, xr[:, :]).then_inc(seq_keys, 1)

        with ExitStack() as ph:
            sqk = sb("sqk", [P, TILE], F32, ph)
            lnk = sb("lnk", [P, TILE], F32, ph)
            rsk = sb("rsk", [P, TILE], F32, ph)
            t_kv = sb("t_kv", [P, 2, 2 * P], F32, ph)
            ek = sb("ek", [P, 2, P], F32, ph)
            gm = sb("gm", [P, P], F32, ph)
            psa = ph.enter_context(nc.psum_tensor("psa", [P, TILE], F32))
            psb = ph.enter_context(nc.psum_tensor("psb", [P, TILE], F32))
            pkv = [ph.enter_context(nc.psum_tensor(f"pkv{j}", [P, 2 * P], F32)) for j in range(2)]
            pg = ph.enter_context(nc.psum_tensor("pg", [P, P], F32))
            psum_k = ph.enter_context(nc.psum_tensor("psum_k", [P, 1], F32))
            pm = ph.enter_context(nc.psum_tensor("pm", [P, P], F32))
            S = lambda n: sem(n, ph)
            kc, ksq, kv_, kln, krs, kn = (S(n) for n in ("k_centered", "k_squared", "k_var", "k_ln", "k_rstd", "k_normed"))
            kvp, kvb_done, kexp, kmap, kvacc, kst, kmm, krelu = (S(n) for n in ("kv_product", "kv_biased", "k_exp", "k_mapped", "kv_summed", "k_step", "k_mm", "k_relu"))
            blk = ph.enter_context(nc.Block())
            KT = NSUB // TILE
            NCH = NSUB // P

            @blk.tensor
            def _(pe):
                for t in range(KT):
                    if t:
                        pe.wait_ge(kn, t)
                    pe.matmul(psa[:, :], center, xsub[:, t * TILE:(t + 1) * TILE], start=True, stop=True).then_inc(kc, 1)
                    pe.wait_ge(ksq, t + 1)
                    pe.matmul(psb[:, :], meanm, sqk[:, :], start=True, stop=True).then_inc(kv_, 1)
                pe.wait_ge(kn, KT)
                for c in range(NCH + 1):
                    if c < NCH:
                        if c >= 2:
                            pe.wait_ge(kvb_done, c - 1)
                        pe.matmul(pkv[c % 2][:, :], xsub[:, c * P:(c + 1) * P], kvT[:, :], start=True,
                                  stop=True).then_inc(kvp, 1)
                    if c:
                        d = c - 1
                        pe.wait_ge(kmap, d + 1)
                        pe.matmul(pg[:, :], t_kv[:, d % 2, P:2 * P], t_kv[:, d % 2, 0:P], start=(d == 0),
                                  stop=(d == NCH - 1))
                        pe.matmul(psum_k[:, :], t_kv[:, d % 2, 0:P], ones[:, :], start=(d == 0),
                                  stop=(d == NCH - 1)).then_inc(kvacc, 1)
                pe.wait_ge(kst, 1)
                pe.matmul(pm[:, :], gm[:, :], pT[:, :], start=True, stop=True).then_inc(kmm, 1)

            @blk.scalar
            def _(act):
                act.preload_act_table_set("natural_log_exp_and_others")
                for t in range(KT):
                    act.wait_ge(kc, t + 1)
                    act.activation(sqk[:, :], psa[:, :], ACT.Square).then_inc(ksq, 1)
                    act.wait_ge(kv_, t + 1)
                    act.activation(lnk[:, :], psb[:, :], ACT.Ln, bias=eps_c).then_inc(kln, 1)
                    act.wait_ge(kln, t + 1)
                    if t:
                        act.wait_ge(kn, t)
                    act.activation(rsk[:, :], lnk[:, :], ACT.Exp, scale=-0.5).then_inc(krs, 1)
                for c in range(NCH):
                    act.wait_ge(kvb_done, c + 1)
                    if c >= 2:
                        act.wait_ge(kmap, c - 1)
                    act.activation(ek[:, c % 2, :], t_kv[:, c % 2, 0:P], ACT.Exp).then_inc(kexp, 1)

            @blk.vector
            def _(dve):
                for t in range(KT):
                    dve.wait_ge(krs, t + 1)
                    dve.tensor_tensor(xsub[:, t * TILE:(t + 1) * TILE], psa[:, :], rsk[:, :], ALU.mult).then_inc(kn, 1)
                for c in range(NCH):
                    dve.wait_ge(kvp, c + 1)
                    if c >= 2:
                        dve.wait_ge(kvacc, c - 1)
                    dve.tensor_tensor(t_kv[:, c % 2, :], pkv[c % 2][:, :], kvb[:, :], ALU.add).then_inc(kvb_done, 1)
                    dve.wait_ge(kexp, c + 1)
                    dve.tensor_scalar(t_kv[:, c % 2, 0:P], t_kv[:, c % 2, 0:P], 0.0, None, ALU.max).then_inc(krelu, 1)
                    dve.wait_ge(krelu, c + 1)
                    dve.scalar_tensor_tensor(out=t_kv[:, c % 2, 0:P], in0=ek[:, c % 2, :], scalar=1.0,
                                             in1=t_kv[:, c % 2, 0:P], op0=ALU.min, op1=ALU.add).then_inc(kmap, 1)
                dve.wait_ge(kvacc, NCH)
                dve.tensor_tensor(gm[:, :], pg[:, :], headm, ALU.mult).then_inc(kst, 1)
                dve.tensor_scalar(dT[:, :], headm, psum_k[:, 0:1], None, ALU.mult).then_inc(kst, 1)
                dve.wait_ge(kmm, 1)
                dve.tensor_copy(mT[:, :], pm[:, :]).then_inc(kst, 1)

        keys.close()
        regions.close()

        tail = ExitStack()
        stack.enter_context(tail)
        w1_sb = sb("w1_sb", [C + 1, E, HID], F32, tail)
        w2_sb = sb("w2_sb", [P, 2, E, C], F32, tail)
        w2b_sb = sb("w2b_sb", [E, C], F32, tail)
        cand = sb("cand", [P, NBLK * K], F32, tail)
        cidx = sb("cidx", [P, NBLK * K], F32, tail)
        ses = sb("ses", [P, NBLK], F32, tail)
        with ExitStack() as ph:
            xb = sb("x2_block", [P, 4, BLOCK], F32, ph)
            x3 = sb("x3_block", [P, 2, BLOCK], F32, ph)
            sq = sb("sq3", [P, 2, TILE], F32, ph)
            ln = sb("ln3", [P, 2, TILE], F32, ph)
            rstd = sb("rstd3", [P, 2, 2, TILE], F32, ph)
            xn = sb("xn3", [P, 2, TILE], F32, ph)
            eq = sb("exp_q", [P, 2, TILE], F32, ph)
            rq = sb("relu_q", [P, 2, TILE], F32, ph)
            qm = sb("q_map", [P, 2, TILE], F32, ph)
            lnd = sb("ln_d", [P, TILE], F32, ph)
            zr = sb("z_inv", [P, 2, TILE], F32, ph)
            qz = sb("q_z", [P, 2, TILE], F32, ph)
            xl4 = sb("xl4", [P, 2, TILE], F32, ph)
            xt = sb("x3_squares", [P, 2, BLOCK], F32, ph)
            lg = sb("logits", [P, 2, BLOCK // 2], F32, ph)
            eg = sb("exp_logits", [P, BLOCK // 2], F32, ph)
            m8 = sb("best8", [P, 2, K], F32, ph)
            i8 = sb("best8_at", [P, 2, K], U32, ph)
            nm = sb("neg_best", [P, 2, 1], F32, ph)
            se = sb("sum_exp", [P, 2, 1], F32, ph)
            pa3, pv3, pq, pd, pm3, pa4, pv4, pgt = (
                ph.enter_context(nc.psum_tensor(n, [P, TILE], F32))
                for n in ("pa3", "pv3", "pq3", "pd3", "pm3", "pa4", "pv4", "pgt"))
            S = lambda n: sem(n, ph)
            x2_loaded = [S(f"x2_loaded{r}") for r in range(4)]
            x3_stored = [S(f"x3_stored{r}") for r in range(2)]
            xt_stored = [S(f"xt_stored{r}") for r in range(2)]
            turned = S("turned")
            w_loaded = S("expert_weights_loaded")
            centered, squared = [S("centered3"), S("centered4")], [S("squared3"), S("squared4")]
            var_ready, ln_done = [S("var_ready3"), S("var_ready4")], [S("ln_done3"), S("ln_done4")]
            rstd_ready, normed = [S("rstd_ready3"), S("rstd_ready4")], [S("normed3"), S("normed4")]
            q_ready, expq_ready, relu_ready, mapped = S("q_ready"), S("expq_ready"), S("relu_ready"), S("mapped")
            d_ready, lnd_done, z_ready, qz_ready = S("d_ready"), S("lnd_done"), S("z_ready"), S("qz_ready")
            m_ready, x3_ready, gated, logits_ready = S("m_ready"), S("x3_ready"), S("gated"), S("logits_ready")
            best_ready, at_ready, neg_ready, expsum_ready, gathered = S("best_ready"), S("at_ready"), S("neg_ready"), S("expsum_ready"), S("gathered")
            blk = ph.enter_context(nc.Block())
            NSLOT = UNROLL * TPB
            LAG = 6

            def schedule(eng, slot):
                for m in range(NSLOT):
                    slot(0, m)
                with eng.Fori(1, NT // NSLOT) as q:
                    for m in range(NSLOT):
                        slot(q, m)
                for m in range(LAG + 1):
                    slot(NT // NSLOT, m)

            def stage(q, m, lag):
                t = NSLOT * q + (m - lag)
                active = not isinstance(t, int) or 0 <= t < NT
                return active, t, (m - lag) // TPB % UNROLL, (m - lag) % TPB

            def past(t, n):
                return not isinstance(t, int) or t >= n

            def cols_of(s):
                return slice(s * TILE, (s + 1) * TILE)

            @blk.sync
            def _(sp):
                def load(k, r):
                    sp.dma_start(xb[:, r, :], x2_d[bass.ds(k, 1), :, :].rearrange("o p n -> p (o n)")).then_inc(x2_loaded[r], 16)

                def store(k, r):
                    sp.wait_ge(x3_ready, 4 * k + 4)
                    sp.dma_start(out_v[:, bass.ds(k * BLOCK, BLOCK)], x3[:, r % 2, :]).then_inc(x3_stored[r % 2], 16)
                    sp.wait_ge(turned, 4 * k + 4)
                    sp.dma_start(xt_d[k, :, :], xt[:, r % 2, :]).then_inc(xt_stored[r % 2], 16)

                for k in range(3):
                    load(k, k)
                sp.dma_start(w1_sb[:, :, :], w1.rearrange("e d h -> d e h")).then_inc(w_loaded, 16)
                for j in range(2):
                    sp.dma_start(w2_sb[:, j, :, :], w2[:, j * P:(j + 1) * P, :].rearrange("e p o -> p e o")).then_inc(w_loaded, 16)
                sp.dma_start(w2b_sb[:, :], w2[:, HID, :]).then_inc(w_loaded, 16)
                for k in range(NBLK):
                    if k >= 1:
                        store(k - 1, (k - 1) % 4)
                    if k + 3 < NBLK:
                        load(k + 3, (k + 3) % 4)
                store(NBLK - 1, (NBLK - 1) % 4)
                for r in range(2):
                    sp.wait_ge(x3_stored[r], 16 * NBLK // 2)
                    sp.wait_ge(xt_stored[r], 16 * NBLK // 2)
                sp.wait_ge(w_loaded, 16 * 4)

            @blk.tensor
            def _(pe):
                def slot(q, m):
                    def center_of(l, lag, bank, src):
                        on, t, r, s = stage(q, m, lag)
                        if on:
                            if l == 0:
                                if s == 0:
                                    pe.wait_ge(x2_loaded[r], 16 * (q + 1))
                            else:
                                pe.wait_ge(x3_ready, t + 1)
                            if past(t, 1):
                                pe.wait_ge(normed[l], t)
                            pe.matmul(bank[:, :], center, src[:, r % (4, 2)[l], cols_of(s)], start=True,
                                      stop=True).then_inc(centered[l], 1)

                    def var_of(l, lag, bank):
                        on, t, r, s = stage(q, m, lag)
                        if on:
                            pe.wait_ge(squared[l], t + 1)
                            if past(t, 1):
                                pe.wait_ge(ln_done[l], t)
                            pe.matmul(bank[:, :], meanm, sq[:, l, :], start=True, stop=True).then_inc(var_ready[l], 1)

                    center_of(0, 0, pa3, xb)
                    on, t, r, s = stage(q, m, 1)
                    if on:
                        pe.wait_ge(normed[0], t + 1)
                        if past(t, 1):
                            pe.wait_ge(mapped, t)
                        pe.matmul(pq[:, :], qT[:, :], xn[:, s % 2, :], start=True, stop=True).then_inc(q_ready, 1)
                    var_of(0, 0, pv3)
                    on, t, r, s = stage(q, m, 2)
                    if on:
                        pe.wait_ge(mapped, t + 1)
                        if past(t, 1):
                            pe.wait_ge(lnd_done, t)
                        pe.matmul(pd[:, :], dT[:, :], qm[:, s % 2, :], start=True, stop=True).then_inc(d_ready, 1)
                    center_of(1, 4, pa4, x3)
                    on, t, r, s = stage(q, m, 3)
                    if on:
                        pe.wait_ge(qz_ready, t + 1)
                        if past(t, 1):
                            pe.wait_ge(x3_ready, t)
                        pe.matmul(pm3[:, :], mT[:, :], qz[:, s % 2, :], start=True, stop=True).then_inc(m_ready, 1)
                    var_of(1, 4, pv4)
                    on, t, r, s = stage(q, m, 5)
                    if on:
                        pe.wait_ge(normed[1], t + 1)
                        if s % 2 == 0:
                            pe.wait_ge(logits_ready, (NSLOT // 2) * q + (m - 5) // 2)
                        pe.matmul(pgt[:, :], gT[:, (s % 2) * P:(s % 2 + 1) * P], xl4[:, s % 2, :],
                                  start=(s % 2 == 0), stop=(s % 2 == 1)).then_inc(gated, 1)
                schedule(pe, slot)

            @blk.scalar
            def _(act):
                act.preload_act_table_set("natural_log_exp_and_others")

                def slot(q, m):
                    def square(l, lag, bank):
                        on, t, r, s = stage(q, m, lag)
                        if on:
                            act.wait_ge(centered[l], t + 1)
                            if past(t, 1):
                                act.wait_ge(var_ready[l], t)
                            act.activation(sq[:, l, :], bank[:, :], ACT.Square).then_inc(squared[l], 1)

                    def rsqrt(l, lag, bank, eps):
                        on, t, r, s = stage(q, m, lag)
                        if on:
                            act.wait_ge(var_ready[l], t + 1)
                            if past(t, 1):
                                act.wait_ge(rstd_ready[l], t)
                            act.activation(ln[:, l, :], bank[:, :], ACT.Ln, bias=eps).then_inc(ln_done[l], 1)
                            act.wait_ge(ln_done[l], t + 1)
                            if past(t, 2):
                                act.wait_ge(normed[l], t - 1)
                            act.activation(rstd[:, l, s % 2, :], ln[:, l, :], ACT.Exp, scale=-0.5).then_inc(rstd_ready[l], 1)

                    square(0, 0, pa3)
                    on, t, r, s = stage(q, m, 1)
                    if on:
                        act.wait_ge(q_ready, t + 1)
                        if past(t, 2):
                            act.wait_ge(mapped, t - 1)
                        act.activation(eq[:, s % 2, :], pq[:, :], ACT.Exp, bias=qb).then_inc(expq_ready, 1)
                    rsqrt(0, 0, pv3, eps_c)
                    on, t, r, s = stage(q, m, 2)
                    if on:
                        act.wait_ge(d_ready, t + 1)
                        if past(t, 1):
                            act.wait_ge(z_ready, t)
                        act.activation(lnd[:, :], pd[:, :], ACT.Ln, bias=eps_z).then_inc(lnd_done, 1)
                        act.wait_ge(lnd_done, t + 1)
                        if past(t, 2):
                            act.wait_ge(qz_ready, t - 1)
                        act.activation(zr[:, s % 2, :], lnd[:, :], ACT.Exp, scale=-1.0).then_inc(z_ready, 1)
                    square(1, 4, pa4)
                    on, t, r, s = stage(q, m, 6)
                    if on and s == TPB - 1:
                        k = UNROLL * q + (m - 6) // TPB
                        act.wait_ge(neg_ready, k + 1)
                        if past(k, 2):
                            act.wait_ge(gathered, k - 1)
                        if past(k, 1):
                            act.wait_ge(expsum_ready, k)
                        act.activation(eg[:, :], lg[:, r % 2, :], ACT.Exp, bias=nm[:, r % 2, :],
                                       accum_out=se[:, r % 2, :]).then_inc(expsum_ready, 1)
                    rsqrt(1, 4, pv4, eps_t)
                schedule(act, slot)

            @blk.gpsimd
            def _(pool):
                with pool.Fori(0, NBLK // 2) as kk2:
                    for r in range(2):
                        k = 2 * kk2 + r
                        pool.wait_ge(at_ready, k + 1)
                        pool.wait_ge(expsum_ready, k + 1)
                        pool.sem_inc(held, 1)
                        pool.tensor_copy(cand[:, bass.ds(k * K, K)], m8[:, r, :])
                        pool.tensor_copy(cidx[:, bass.ds(k * K, K)], i8[:, r, :])
                        pool.tensor_copy(ses[:, bass.ds(k, 1)], se[:, r, :]).then_inc(gathered, 1)

            @blk.vector
            def _(dve):
                def slot(q, m):
                    on, t, r, s = stage(q, m, 1)
                    if on:
                        dve.wait_ge(expq_ready, t + 1)
                        dve.tensor_scalar(rq[:, s % 2, :], pq[:, :], qb, 0.0, ALU.add, ALU.max).then_inc(relu_ready, 1)
                        dve.wait_ge(relu_ready, t + 1)
                        if past(t, 2):
                            dve.wait_ge(d_ready, t - 1)
                        dve.scalar_tensor_tensor(out=qm[:, s % 2, :], in0=eq[:, s % 2, :], scalar=1.0,
                                                 in1=rq[:, s % 2, :], op0=ALU.min, op1=ALU.add).then_inc(mapped, 1)
                    on, t, r, s = stage(q, m, 0)
                    if on:
                        dve.wait_ge(rstd_ready[0], t + 1)
                        if past(t, 2):
                            dve.wait_ge(q_ready, t - 1)
                        dve.tensor_tensor(xn[:, s % 2, :], pa3[:, :], rstd[:, 0, s % 2, :], ALU.mult).then_inc(normed[0], 1)
                    on, t, r, s = stage(q, m, 2)
                    if on:
                        dve.wait_ge(mapped, t + 1)
                        dve.wait_ge(z_ready, t + 1)
                        if past(t, 2):
                            dve.wait_ge(m_ready, t - 1)
                        dve.tensor_tensor(qz[:, s % 2, :], qm[:, s % 2, :], zr[:, s % 2, :], ALU.mult).then_inc(qz_ready, 1)
                    on, t, r, s = stage(q, m, 3)
                    if on:
                        dve.wait_ge(m_ready, t + 1)
                        k = UNROLL * q + (m - 3) // TPB
                        if s == 0 and past(k, 2):
                            dve.wait_ge(centered[1], 4 * k - 4)
                            dve.wait_ge(turned, 4 * k - 4)
                            dve.wait_ge(x3_stored[r % 2], 16 * (2 * q + (m - 3) // (2 * TPB)))
                        dve.scalar_tensor_tensor(out=x3[:, r % 2, cols_of(s)], in0=pm3[:, :], scalar=pb,
                                                 in1=xb[:, r, cols_of(s)], op0=ALU.add, op1=ALU.add).then_inc(x3_ready, 1)
                    on, t, r, s = stage(q, m, 5)
                    if on and s % 2 == 1:
                        pair = s // 2
                        k = UNROLL * q + (m - 5) // TPB
                        dve.wait_ge(gated, t + 1)
                        if pair == 0 and past(k, 2):
                            dve.wait_ge(expsum_ready, k - 1)
                        dve.tensor_scalar(lg[:, r % 2, pair * TILE:(pair + 1) * TILE], pgt[:, :], gb, None,
                                          ALU.add).then_inc(logits_ready, 1)
                        if pair == 1:
                            dve.wait_ge(logits_ready, 2 * k + 2)
                            if past(k, 2):
                                dve.wait_ge(gathered, k - 1)
                            dve.sem_inc(held, 1)
                            dve.max(m8[:, r % 2, :], lg[:, r % 2, :]).then_inc(best_ready, 1)
                            dve.wait_ge(best_ready, k + 1)
                            dve.sem_inc(held, 1)
                            dve.max_index(i8[:, r % 2, :], m8[:, r % 2, :], lg[:, r % 2, :]).then_inc(at_ready, 1)
                            dve.tensor_scalar(nm[:, r % 2, :], m8[:, r % 2, 0:1], -1.0, None, ALU.mult).then_inc(neg_ready, 1)
                    on, t, r, s = stage(q, m, 4)
                    if on:
                        dve.wait_ge(rstd_ready[1], t + 1)
                        if past(t, 2):
                            dve.wait_ge(gated, t - 1)
                        dve.tensor_tensor(xl4[:, s % 2, :], pa4[:, :], rstd[:, 1, s % 2, :], ALU.mult).then_inc(normed[1], 1)
                    on, t, r, s = stage(q, m, 4)
                    if on:
                        k = UNROLL * q + (m - 4) // TPB
                        dve.wait_ge(x3_ready, t + 1)
                        if s == 0 and past(k, 2):
                            dve.wait_ge(xt_stored[r % 2], 16 * (2 * q + (m - 4) // (2 * TPB)))
                        dve.transpose(xt[:, r % 2, cols_of(s)], x3[:, r % 2, cols_of(s)]).then_inc(turned, 1)
                schedule(dve, slot)

        with ExitStack() as ph:
            NC = NBLK * K
            c2 = sb("c2", [64, 2 * NC], F32, ph)
            i2 = sb("i2", [64, 2 * NC], F32, ph)
            se2 = sb("se2", [64, 2 * NBLK], F32, ph)
            ex = sb("ex", [64, 2 * NBLK], F32, ph)
            jk = sb("jk", [64, 2 * NC], F32, ph)
            t8 = sb("t8", [64, K], F32, ph)
            a8 = sb("a8", [64, K], U32, ph)
            a8f = sb("a8f", [64, K], F32, ph)
            nmx = sb("nmx", [64, 4], F32, ph)
            tokf = sb("tokf", [64, K], F32, ph)
            toki = sb("toki", [64, K], I32, ph)
            prob = sb("prob", [64, K], F32, ph)
            half = sb("half_of_pair", [P, NC], F32, ph)
            toki2 = sb("token_of_slot", [P, B, 2], I32, ph)
            row_terms = sb("row_terms", [P, 3, B, 2], I32, ph)
            row0 = sb("row_of_slot", [P, B, 2], I32, ph)
            row_at = sb("row_at", [P, 2, B, 2], I32, ph)
            xs = sb("x3_of_slot", [P, 2, P], F32, ph)
            eq_later = sb("eq_later", [P, B, 2, E * K], F32, ph)
            wide_ones = sb("wide_ones", [P, C], F32, ph)
            tokq = sb("token_by_channel", [P, E * K], F32, ph)
            repeat = sb("repeat", [P, E * K], F32, ph)
            word = sb("word_of_slot", [P, E * K], I32, ph)
            NS = E * K
            tokr = sb("tokr", [P, B, NS], F32, ph)
            tokc = sb("tokc", [P, B, 2], F32, ph)
            pr = sb("pr", [P, NS], F32, ph)
            xg = sb("xg", [P, NS], F32, ph)
            sqg = sb("sqg", [P, NS], F32, ph)
            lng = sb("lng", [P, NS], F32, ph)
            xgn = sb("xgn", [P, NS], F32, ph)
            pool_sb = sb("pool_sb", [P, E], F32, ph)
            hin = sb("hin", [C + 1, B, E], F32, ph)
            h1 = sb("h1", [P, 2, E, B], F32, ph)
            o_sb = sb("o_sb", [C, E, B], F32, ph)
            wv = sb("wv", [P, NS], F32, ph)
            wvT = sb("wvT", [P, 2, P], F32, ph)
            eqm = sb("eqm", [P, B, 2, NS], F32, ph)
            fin = sb("fin", [P, NS], F32, ph)
            pgn = ph.enter_context(nc.psum_tensor("pgn", [P, NS], F32))
            pgv = ph.enter_context(nc.psum_tensor("pgv", [P, NS], F32))
            php = ph.enter_context(nc.psum_tensor("php", [C, B, E], F32))
            pgx, prep = pgv, pgn
            ph1 = ph.enter_context(nc.psum_tensor("ph1", [P, 2, E, B], F32))
            po = ph.enter_context(nc.psum_tensor("po", [C, E, B], F32))
            po2 = ph.enter_context(nc.psum_tensor("po2", [P, E], F32))
            pt = ph.enter_context(nc.psum_tensor("pt", [P, 2, P], F32))
            pc = ph.enter_context(nc.psum_tensor("pc", [P, NS], F32))
            S = lambda n: sem(n, ph)
            placed, merged, out_tok, back, dv, ac, mm, gath, scat = (
                S(n) for n in ("placed", "merged", "tokens_out", "tokens_back", "tail_vector", "tail_scalar", "tail_tensor", "columns_in", "columns_out"))
            gp = S("tail_pool")
            back2, rep, turned_back = S("broadcasts_back"), S("repeats_counted"), S("tokens_turned")
            blk = ph.enter_context(nc.Block())
            ONE = dict(allow_slow_non_contiguous=True)

            SKIP = float(2 ** 28)
            out_words = out.rearrange("b c h w -> (b c h w)").rearrange("(n o) -> n o", o=1)
            xt_rows = xt_d.rearrange("k p (m j) -> (k p m) j", j=32)

            @blk.sync
            def _(sp):
                sp.wait_ge(placed, 1)
                for j in range(2):
                    rows = slice(j * 64, (j + 1) * 64)
                    sp.dma_start(c2[:, j * NC:(j + 1) * NC], cand[rows, :]).then_inc(merged, 16)
                    sp.dma_start(i2[:, j * NC:(j + 1) * NC], cidx[rows, :]).then_inc(merged, 16)
                    sp.dma_start(se2[:, j * NBLK:(j + 1) * NBLK], ses[rows, :]).then_inc(merged, 16)
                sp.wait_ge(dv, DV_TOK)
                sp.dma_start(tok_d.rearrange("(p k) -> p k", k=K), toki[:, :]).then_inc(out_tok, 16)
                sp.dma_start(tokf_d.rearrange("(p k) -> p k", k=K), tokf[:, :]).then_inc(out_tok, 16)
                sp.dma_start(prob_d.rearrange("(p k) -> p k", k=K), prob[:, :]).then_inc(out_tok, 16)
                sp.wait_ge(out_tok, 48)
                sp.dma_start(toki2[:, :, :].rearrange("p b j -> p (b j)"), tok_d.rearrange("(n p) -> p n", p=P), **ONE).then_inc(back, 16)
                sp.dma_start(tokc[:, :, :].rearrange("p b j -> p (b j)"), tokf_d.rearrange("(n p) -> p n", p=P), **ONE).then_inc(back2, 16)
                for b in range(B):
                    rows = slice(b * C, (b + 1) * C)
                    sp.dma_start(tokr[:, b, :], tokf_d[b * NS:(b + 1) * NS].partition_broadcast(P)).then_inc(back2, 16)
                    sp.dma_start(tokq[rows, :], tokf_d[b * NS:(b + 1) * NS].partition_broadcast(C)).then_inc(back2, 16)
                    sp.dma_start(pr[rows, :], prob_d[b * NS:(b + 1) * NS].partition_broadcast(C)).then_inc(back2, 16)
                sp.wait_ge(back2, 16 * 7)

            @blk.scalar
            def _(act):
                act.preload_act_table_set("natural_log_exp_and_others")
                act.wait_ge(dv, DV_MAX)
                act.activation(ex[:, :], c2[:, ::K], ACT.Exp, bias=nmx[:, 0:1]).then_inc(ac, 1)
                act.activation(prob[:, :], t8[:, :], ACT.Exp, bias=nmx[:, 0:1]).then_inc(ac, 1)
                act.wait_ge(mm, 1)
                act.activation(sqg[:, :], pgn[:, :], ACT.Square).then_inc(ac, 1)
                act.wait_ge(mm, 2)
                act.activation(lng[:, :], pgv[:, :], ACT.Ln, bias=eps_t).then_inc(ac, 1)
                act.wait_ge(ac, 4)
                act.activation(lng[:, :], lng[:, :], ACT.Exp, scale=-0.5).then_inc(ac, 1)
                act.preload_act_table(ACT.Gelu)
                act.wait_ge(mm, 4)
                act.activation(h1[:, :, :, :].rearrange("p j e b -> p (j e b)"),
                               ph1[:, :, :, :].rearrange("p j e b -> p (j e b)"), ACT.Gelu).then_inc(ac, 1)

            @blk.gpsimd
            def _(pool):
                pool.memset(hin[C:C + 1, :, :], 1.0).then_inc(gp, 1)
                pool.wait_ge(gp, 1)
                pool.memset(wide_ones[:, :], 1.0).then_inc(gp, 1)
                pool.wait_ge(dv, DV_ROWS)
                for h in range(2):
                    for b in range(B):
                        for j in range(2):
                            pool.indirect_dma_start(
                                out=xs[:, j, b * C + h * 32:b * C + h * 32 + 32], out_offset=None, in_=xt_rows,
                                in_offset=bass.IndirectOffsetOnAxis(ap=row_at[:, h, b, j:j + 1], axis=0)).then_inc(gath, 16)
                pool.wait_ge(dv, DV_FIN)
                for s in range(NS):
                    pool.indirect_dma_start(
                        out=out_words, out_offset=bass.IndirectOffsetOnAxis(ap=word[:, s:s + 1], axis=0),
                        in_=fin[:, s:s + 1], in_offset=None, bounds_check=B * C * N - 1,
                        oob_is_err=False).then_inc(scat, 16)
                pool.wait_ge(scat, 16 * NS)

            n_dv = [0]

            @blk.tensor
            def _(pe):
                pe.wait_ge(gp, 2)
                pe.wait_ge(dv, DV_EQ)
                for b in range(B):
                    for j in range(2):
                        m = pe.matmul(prep[b * C:(b + 1) * C, :], wide_ones[:, :], eq_later[:, b, j, :],
                                      start=(j == 0), stop=(j == 1))
                m.then_inc(rep, 1)
                pe.wait_ge(gath, 16 * 8)
                for j in range(2):
                    m = pe.transpose(pgx[:, j * P:(j + 1) * P], xs[:, j, :], ident)
                m.then_inc(turned_back, 1)
                pe.wait_ge(dv, DV_XG)
                pe.matmul(pgn[:, :], center, xg[:, :], start=True, stop=True).then_inc(mm, 1)
                pe.wait_ge(ac, 3)
                pe.matmul(pgv[:, :], meanm, sqg[:, :], start=True, stop=True).then_inc(mm, 1)
                pe.wait_ge(dv, DV_POOL)
                for b in range(B):
                    m = pe.matmul(php[:, b, :], ident[:, b * C:(b + 1) * C], pool_sb[:, :], start=True, stop=True)
                m.then_inc(mm, 1)
                pe.wait_ge(dv, DV_HIN)
                pe.wait_ge(gp, 1)
                for e in range(E):
                    for j in range(2):
                        m = pe.matmul(ph1[:, j, e, :], w1_sb[:, e, j * P:(j + 1) * P], hin[:, :, e],
                                      start=True, stop=True)
                m.then_inc(mm, 1)
                pe.wait_ge(ac, 6)
                pe.matmul(po[:, :, :], w2b_sb[:, :], ident[0:E, 0:E].unsqueeze(2).to_broadcast([E, E, B]), start=True,
                          stop=False, skip_group_check=True)
                for e in range(E):
                    for j in range(2):
                        m = pe.matmul(po[:, e, :], w2_sb[:, j, e, :], h1[:, j, e, :], start=False,
                                      stop=(j == 1), skip_group_check=True)
                m.then_inc(mm, 1)
                pe.wait_ge(dv, DV_OUT)
                for b in range(B):
                    m = pe.matmul(po2[b * C:(b + 1) * C, :], ident[0:C, 0:C], o_sb[:, :, b], start=True, stop=True)
                m.then_inc(mm, 1)
                pe.wait_ge(dv, DV_WV)
                for j in range(2):
                    m = pe.transpose(pt[:, j, :], wv[:, j * P:(j + 1) * P], ident)
                m.then_inc(mm, 1)
                pe.wait_ge(dv, DV_WVT)
                for b in range(B):
                    for j in range(2):
                        m = pe.matmul(pc[b * C:(b + 1) * C, :], wvT[:, j, b * C:(b + 1) * C], eqm[:, b, j, :],
                                      start=(j == 0), stop=(j == 1))
                m.then_inc(mm, 1)

            @blk.vector
            def _(dve):
                did = n_dv

                def go(ins):
                    did[0] += 1
                    ins.then_inc(dv, 1)
                    dve.wait_ge(dv, did[0])

                go(dve.tensor_scalar(half[:, :], cidx[:, :], float(TILE), float(TILE), ALU.is_ge, ALU.mult))
                go(dve.tensor_tensor(half[:, :], half[:, :], base_c, ALU.add))
                dve.tensor_tensor(cidx[:, :], cidx[:, :], half[:, :], ALU.add).then_inc(placed, 1)
                dve.wait_ge(merged, 96)
                go(dve.max(t8[:, :], c2[:, :]))
                go(dve.tensor_scalar(nmx[:, 0:1], t8[:, 0:1], -1.0, None, ALU.mult))
                assert did[0] == DV_MAX
                go(dve.max_index(a8[:, :], t8[:, :], c2[:, :]))
                go(dve.tensor_copy(a8f[:, :], a8[:, :]))
                for k in range(K):
                    go(dve.scalar_tensor_tensor(out=jk[:, :], in0=iota_c[0:64, :], scalar=a8f[:, k:k + 1],
                                                in1=i2[:, :], op0=ALU.is_equal, op1=ALU.mult,
                                                accum_out=tokf[:, k:k + 1]))
                go(dve.tensor_copy(toki[:, :], tokf[:, :]))
                dve.wait_ge(ac, 2)
                go(dve.scalar_tensor_tensor(out=jk[:, 0:2 * NBLK], in0=ex[:, :], scalar=1.0, in1=se2[:, :],
                                            op0=ALU.mult, op1=ALU.mult, accum_out=nmx[:, 1:2]))
                go(dve.reciprocal(nmx[:, 2:3], nmx[:, 1:2]))
                go(dve.tensor_scalar(prob[:, :], prob[:, :], nmx[:, 2:3], None, ALU.mult))
                assert did[0] == DV_TOK
                dve.wait_ge(back, 16)
                for i, (op0, n0, op1, n1) in enumerate((
                        (ALU.logical_shift_right, 11, ALU.logical_shift_left, 13),
                        (ALU.bitwise_and, 31, ALU.logical_shift_left, 6),
                        (ALU.logical_shift_right, 5, ALU.bitwise_and, 63))):
                    go(dve.tensor_scalar(row_terms[:, i, :, :], toki2[:, :, :], n0, n1, op0, op1))
                go(dve.tensor_tensor(row0[:, :, :], row_terms[:, 0, :, :], row_terms[:, 1, :, :], ALU.add))
                go(dve.tensor_tensor(row0[:, :, :], row0[:, :, :], row_terms[:, 2, :, :], ALU.add))
                for h in range(2):
                    for b in range(B):
                        go(dve.tensor_scalar(row_at[:, h, b, :], row0[:, b, :], float((2 * b + h) * BLOCK), None, ALU.add))
                assert did[0] == DV_ROWS
                dve.wait_ge(back2, 16 * 7)
                for b in range(B):
                    for j in range(2):
                        go(dve.tensor_scalar(eqm[:, b, j, :], tokr[:, b, :], tokc[:, b, j:j + 1], None, ALU.is_equal))
                        go(dve.tensor_tensor(eq_later[:, b, j, :], eqm[:, b, j, :], later[:, j, :], ALU.mult))
                assert did[0] == DV_EQ
                dve.wait_ge(rep, 1)
                go(dve.tensor_scalar(repeat[:, :], prep[:, :], 0.0, SKIP, ALU.is_gt, ALU.mult))
                go(dve.scalar_tensor_tensor(out=word[:, :], in0=tokq[:, :], scalar=start_c, in1=repeat[:, :],
                                            op0=ALU.add, op1=ALU.add))
                dve.wait_ge(turned_back, 1)
                go(dve.tensor_copy(xg[:, :], pgx[:, :]))
                assert did[0] == DV_XG
                dve.wait_ge(ac, 5)
                go(dve.tensor_tensor(xgn[:, :], pgn[:, :], lng[:, :], ALU.mult))
                go(dve.tensor_tensor(xgn[:, :], xgn[:, :], pr[:, :], ALU.mult))
                go(dve.tensor_reduce(pool_sb[:, :], xgn[:, :].rearrange("p (e k) -> p e k", k=K), AX.X, ALU.add))
                assert did[0] == DV_POOL
                dve.wait_ge(mm, 3)
                go(dve.tensor_copy(hin[0:C, :, :], php[:, :, :]))
                assert did[0] == DV_HIN
                dve.wait_ge(mm, 5)
                go(dve.tensor_copy(o_sb[:, :, :], po[:, :, :]))
                assert did[0] == DV_OUT
                dve.wait_ge(mm, 6)
                go(dve.tensor_tensor(wv[:, :].rearrange("p (e k) -> p e k", k=K),
                                     pr[:, :].rearrange("p (e k) -> p e k", k=K),
                                     po2[:, :].unsqueeze(2).to_broadcast([P, E, K]), ALU.mult))
                assert did[0] == DV_WV
                dve.wait_ge(mm, 7)
                go(dve.tensor_copy(wvT[:, :, :], pt[:, :, :]))
                assert did[0] == DV_WVT
                dve.wait_ge(mm, 8)
                go(dve.tensor_tensor(fin[:, :], xg[:, :], pc[:, :], ALU.add))
                assert did[0] == DV_FIN


DV_MAX = 4
DV_TOK = DV_MAX + 2 + K + 1 + 3
DV_ROWS = DV_TOK + 3 + 2 + 4
DV_EQ = DV_ROWS + 2 * 4
DV_XG = DV_EQ + 2 + 1
DV_POOL = DV_XG + 3
DV_HIN = DV_POOL + 1
DV_OUT = DV_HIN + 1
DV_WV = DV_OUT + 1
DV_WVT = DV_WV + 1
DV_FIN = DV_WVT + 1

_INS = ["x", "L0_conv_kernel", "L0_ffn_W", "L0_ffn_V", "L0_ffn_gamma", "L0_ffn_beta", "L1_conv_q_w",
        "L1_conv_q_b", "L1_conv_kv_w", "L1_conv_kv_b", "L1_conv_proj_w", "L1_conv_proj_b",
        "L1_ffn_gate_w", "L1_ffn_gate_b", "L1_ffn_weight1", "L1_ffn_weight2"]


def kernel(**inputs):
    import concourse.bacc as bacc
    from concourse.bass_utils import run_bass_kernel_spmd

    nc = bacc.Bacc("TRN2", target_bir_lowering=False, num_devices=1)
    arrays, args = {}, []
    for name, a in [(n, inputs[n]) for n in _INS] + [("constants", constants())]:
        a = np.ascontiguousarray(a)
        arrays[f"in_{name}"] = a
        args.append(nc.dram_tensor(f"in_{name}", a.shape, mybir.dt.from_np(a.dtype), kind="ExternalInput").ap())
    args.append(nc.dram_tensor("out_0", (B, C, H, W), F32, kind="ExternalOutput").ap())
    build_program(nc, *args)
    r = run_bass_kernel_spmd(nc, [arrays], core_ids=[0])
    return r.results[0]["out_0"]
```

```python
from contextlib import ExitStack

import numpy as np

import concourse.bass as bass
from concourse import mybir

F32 = mybir.dt.float32
I32 = mybir.dt.int32
U32 = mybir.dt.uint32
ALU = mybir.AluOpType
ACT = mybir.ActivationFunctionType
AX = mybir.AxisListType

B, C, H, W = 2, 64, 256, 256
P = B * C
N = H * W
TILE = 512
BLOCK = 2048
TPB = BLOCK // TILE
NBLK = N // BLOCK
NT = N // TILE
ROWS = BLOCK // W
RPT = TILE // W
UNROLL = 4
HEADS, HD = 8, 8
EPS_C, EPS_T, EPS_BN, EPS_Z = 1e-6, 1e-5, 1e-5, 1e-6
E, K, HID = 32, 8, 256
SUB, SUB0 = 4, 2
NSUB = (H // SUB) * (W // SUB)
SUBB = NSUB // NBLK

REGIONS = 4
RLEN = N // REGIONS
CHUNKS = 512
CLEN = RLEN // CHUNKS
WARM = 12
STEPS = WARM + CLEN
RBLK = RLEN // BLOCK
STATE_TOL = 5e-7


def constants():
    eye = np.eye(P)
    same_batch = np.kron(np.eye(B), np.ones((C, C)))
    mean = same_batch / C
    heads = np.kron(np.eye(B * HEADS), np.ones((HD, HD)))
    pair = np.kron(np.ones((B, B)), np.eye(C)) / B
    base = np.zeros((P, NBLK * K))
    for blk in range(NBLK):
        base[:64, blk * K:(blk + 1) * K] = blk * BLOCK
        base[64:, blk * K:(blk + 1) * K] = blk * BLOCK + TILE
    iota = np.tile(np.arange(2 * NBLK * K), (P, 1))
    slot = np.arange(E * K)
    later = [slot[None] > half * P + np.arange(P)[:, None] for half in range(2)]
    start = np.arange(P)[:, None] * N
    return np.concatenate([eye, mean, eye - mean, heads, pair, base, iota] + later + [start], 1).astype(np.float32)


def build_program(nc, x, conv_k, ffn_w, ffn_v, gamma, beta, q_w, q_b, kv_w, kv_b, proj_w, proj_b,
                  gate_w, gate_b, w1, w2, const, out, debug=None):
    stack = ExitStack()
    with stack:
        def sb(name, shape, dt=F32, where=stack):
            return where.enter_context(nc.sbuf_tensor(name, shape, dt))

        def sem(name, where):
            return where.enter_context(nc.semaphore(name))

        def dram(name, shape, dt=F32):
            return nc.dram_tensor(name, shape, dt, kind="Internal").ap()

        held = sem("held", stack)

        x1_d = dram("x1_scratch", (NBLK, P, BLOCK))
        xl_d = dram("xl_scratch", (NBLK, P, BLOCK))
        x2_d = dram("x2_scratch", (NBLK, P, BLOCK))
        tok_d = dram("token_scratch", (B * E * K,), I32)
        tokf_d = dram("token_f_scratch", (B * E * K,))
        prob_d = dram("prob_scratch", (B * E * K,))
        xt_d = dram("x3_transposed", (NBLK, P, BLOCK))
        x_v = x.rearrange("b c h w -> (b c) (h w)")
        out_v = out.rearrange("b c h w -> (b c) (h w)")

        cst = sb("cst", list(const.shape))
        ident, meanm, center, headm, pairm = (cst[:, i * P:(i + 1) * P] for i in range(5))
        base_c = cst[:, 5 * P:5 * P + NBLK * K]
        iota_c = cst[:, 5 * P + NBLK * K:5 * P + 3 * NBLK * K]
        later = cst[:, 5 * P + 3 * NBLK * K:5 * P + 3 * NBLK * K + 2 * E * K].rearrange("p (j s) -> p j s", j=2)
        start_c = cst[:, 5 * P + 3 * NBLK * K + 2 * E * K:]
        wT = sb("wT", [P, P])
        vT = sb("vT", [P, P])
        qT = sb("qT", [P, P])
        pT = sb("pT", [P, P])
        w_rows = sb("w_rows", [P, P])
        gateT = sb("gateT", [P, 2 * P])
        pair_mean = sb("pair_mean", [P, 3 * 64])
        kvT = sb("kvT", [P, 2 * P])
        kvb = sb("kvb", [P, 2 * P])
        kk = sb("kk", [P, 9])
        cols = sb("cols", [P, 8])
        qb, pb, gb, gam, bet, eps_c, eps_t, eps_z = (cols[:, i:i + 1] for i in range(8))
        taps = sb("taps", [P, P])
        stats = sb("stats", [P, NT, 6])
        bn = sb("bn", [P, 8])
        ones = sb("ones", [P, 1])
        dT = sb("dT", [P, P])
        mT = sb("mT", [P, P])

        PE_TAPS = [4]
        ACT_TAPS = [0, 2, 8]
        DVE_TAPS = [1, 3, 5, 6, 7]

        with ExitStack() as ph:
            src = {n: sb(f"src_{n}", [P, P], F32, ph) for n in ("v", "q", "p", "g", "kv0", "kv1")}
            tp = [ph.enter_context(nc.psum_tensor(f"tp{i}", [P, P], F32)) for i in range(8)]
            gate_rows = sb("gate_rows", [P, 64], F32, ph)
            zeroed, loaded, vectors_loaded, transposed, copied, gate_turned = (
                sem(n, ph) for n in ("zeroed", "loaded", "vectors_loaded", "transposed", "copied", "gate_turned"))
            blk = ph.enter_context(nc.Block())

            @blk.gpsimd
            def _(pool):
                for t in (w_rows, src["v"], src["q"], src["p"], src["g"], src["kv0"], src["kv1"]):
                    pool.memset(t[:, :], 0.0).then_inc(zeroed, 1)
                pool.memset(eps_c, EPS_C).then_inc(zeroed, 1)
                pool.memset(eps_t, EPS_T).then_inc(zeroed, 1)
                pool.memset(eps_z, EPS_Z).then_inc(zeroed, 1)
                pool.memset(ones[:, :], 1.0).then_inc(zeroed, 1)
                pool.memset(pair_mean[:, :], 0.0).then_inc(zeroed, 1)
                for b in range(B):
                    d = slice(b * C, (b + 1) * C)
                    for col, vec in ((qb, q_b), (pb, proj_b), (gam, gamma), (bet, beta)):
                        pool.dma_start(col[d, :], vec.rearrange("(c o) -> c o", o=1)).then_inc(vectors_loaded, 16)
                for r in range(4):
                    pool.dma_start(gb[r * E:(r + 1) * E, :], gate_b.rearrange("(c o) -> c o", o=1)).then_inc(vectors_loaded, 16)

            @blk.sync
            def _(sp):
                sp.dma_start(cst[:, :], const).then_inc(loaded, 16)
                sp.wait_ge(zeroed, 7)
                for b in range(B):
                    d = slice(b * C, (b + 1) * C)
                    sp.dma_start(w_rows[d, d], ffn_w).then_inc(loaded, 16)
                    sp.dma_start(src["v"][d, d], ffn_v).then_inc(loaded, 16)
                    sp.dma_start(src["q"][d, d], q_w).then_inc(loaded, 16)
                    sp.dma_start(src["p"][d, d], proj_w).then_inc(loaded, 16)
                    sp.dma_start(src["g"][b * E:(b + 1) * E, d], gate_w).then_inc(loaded, 16)
                    sp.dma_start(src[f"kv{b}"][:, d], kv_w).then_inc(loaded, 16)
                    sp.dma_start(kk[d, :], conv_k.rearrange("c o i j -> c (o i j)")).then_inc(loaded, 16)
                    for part in range(2):
                        row = kv_b[part * C:(part + 1) * C].partition_broadcast(P)
                        sp.dma_start(kvb[:, part * P + b * C:part * P + (b + 1) * C], row).then_inc(loaded, 16)
                sp.wait_ge(loaded, 16 * (1 + 2 * 9))
                sp.wait_ge(vectors_loaded, 16 * (2 * 4 + 4))

            @blk.tensor
            def _(pe):
                pe.wait_ge(loaded, 16 * (1 + 2 * 9))
                order = (w_rows, src["v"], src["q"], src["p"], src["g"], src["kv0"], src["kv1"])
                for i, m in enumerate(order):
                    pe.transpose(tp[i][:, :], m[:, :], ident).then_inc(transposed, 1)
                pe.wait_ge(gate_turned, 1)
                pe.matmul(tp[7][:, 0:64], center, gate_rows[:, :], start=True, stop=True).then_inc(transposed, 1)

            @blk.vector
            def _(dve):
                dve.wait_ge(zeroed, 12)
                dve.wait_ge(transposed, 7)
                dve.tensor_copy(gate_rows[:, :], tp[4][:, 0:64]).then_inc(gate_turned, 1)
                for i, t in enumerate((wT, vT, qT, pT)):
                    dve.tensor_copy(t[:, :], tp[i][:, :]).then_inc(copied, 1)
                dve.wait_ge(transposed, 8)
                dve.tensor_copy(gateT[:, 0:64], tp[7][:, 0:64]).then_inc(copied, 1)
                dve.tensor_copy(gateT[:, P + 64:2 * P], tp[7][:, 0:64]).then_inc(copied, 1)
                for b in range(B):
                    for to in (gateT[:, 64:P], gateT[:, P:P + 64], pair_mean[:, 64:P]):
                        dve.tensor_copy(to[:, b * E:(b + 1) * E], meanm[:, b * C:b * C + E]).then_inc(copied, 1)
                for b in range(B):
                    for part in range(2):
                        dve.tensor_copy(kvT[:, part * P + b * C:part * P + (b + 1) * C],
                                        tp[5 + b][:, part * C:(part + 1) * C]).then_inc(copied, 1)
                for i, t in enumerate(PE_TAPS):
                    dve.tensor_scalar(taps[:, i * P:(i + 1) * P], ident, kk[:, t:t + 1], None,
                                      ALU.mult).then_inc(copied, 1)

        regions = ExitStack()
        stack.enter_context(regions)
        XL = [sb("region0", [P, WARM + RLEN], F32, regions)]

        with ExitStack() as ph:
            PITCH = W + 2
            xin = sb("xin", [P, 4, BLOCK], F32, ph)
            xn = sb("xn", [P, 2, ROWS + 2, PITCH], F32, ph)
            x1 = sb("x1", [P, 2, BLOCK], F32, ph)
            xl = sb("xl", [P, 2, BLOCK], F32, ph)
            acc = sb("acc", [P, 2, RPT, W], F32, ph)
            sq = sb("sq", [P, 2, TILE], F32, ph)
            ln = sb("ln", [P, 2, TILE], F32, ph)
            rstd = sb("rstd", [P, 2, 2, TILE], F32, ph)
            zero_row = sb("zero_row", [P, W], F32, ph)
            prod = sb("tap_products", [P, len(ACT_TAPS), RPT, W], F32, ph)
            xr = sb("x_and_products", [P, 2, TILE], F32, ph)
            psc = [[ph.enter_context(nc.psum_tensor(f"psc{l}{j}", [P, TILE], F32)) for j in range(2)] for l in range(2)]
            psv = [ph.enter_context(nc.psum_tensor(f"psv{l}", [P, TILE], F32)) for l in range(2)]
            pst = ph.enter_context(nc.psum_tensor("pst", [P, TILE], F32))
            psw = ph.enter_context(nc.psum_tensor("psw", [P, TILE], F32))
            S = lambda n: sem(n, ph)
            x_loaded = [S(f"x_loaded{r}") for r in range(4)]
            x1_stored = [S(f"x1_stored{r}") for r in range(2)]
            xl_stored = [S(f"xl_stored{r}") for r in range(2)]
            centered = [S("centered1"), S("centered2")]
            squared = [S("squared1"), S("squared2")]
            var_ready = [S("var_ready1"), S("var_ready2")]
            ln_done = [S("ln_done1"), S("ln_done2")]
            rstd_ready = [S("rstd_ready1"), S("rstd_ready2")]
            normed = [S("normed1"), S("normed2")]
            pads_ready = S("pads_ready")
            halo_ready = S("halo_ready")
            taps_ready = S("taps_ready")
            acc_step = S("acc_step")
            products = S("products")
            product_added = S("product_added")
            x1_ready = S("x1_ready")
            region0_loaded = S("region0_loaded")
            wx_ready = S("wx_ready")
            bn_done = S("bn_done")
            blk = ph.enter_context(nc.Block())
            NACC, NPROD = len(DVE_TAPS), len(ACT_TAPS)
            LAG = 3

            def schedule(eng, iteration):
                for u in range(UNROLL):
                    iteration(0, u)
                with eng.Fori(1, NBLK // UNROLL) as q:
                    for u in range(UNROLL):
                        iteration(q, u)
                for u in range(LAG):
                    iteration(NBLK // UNROLL, u)

            def stage(q, u, lag):
                k = 4 * q + (u - lag)
                active = not isinstance(k, int) or 0 <= k < NBLK
                return active, k, (u - lag) % 4

            def rounds(q, u, lag, ring):
                return (4 // ring) * q + (u - lag) // ring

            def tile_cols(s):
                return slice(s * TILE, (s + 1) * TILE)

            @blk.sync
            def _(sp):
                def load(q, u, lead):
                    on, k, r = stage(q, u, -lead)
                    if not on:
                        return
                    if not isinstance(k, int) or k >= 4:
                        sp.wait_ge(x1_ready, 4 * k - 12)
                    sp.dma_start(xin[:, r, :], x_v[:, bass.ds(k * BLOCK, BLOCK)]).then_inc(x_loaded[r], 16)

                def iteration(q, u):
                    load(q, u, 2)
                    on, k, r = stage(q, u, 1)
                    if on:
                        sp.wait_ge(x1_ready, 4 * k + 4)
                        sp.dma_start(x1_d[bass.ds(k, 1), :, :].rearrange("o p n -> p (o n)"),
                                     x1[:, r % 2, :]).then_inc(x1_stored[r % 2], 16)
                    on, k, r = stage(q, u, 2)
                    if on:
                        sp.wait_ge(normed[1], 4 * k + 4)
                        sp.dma_start(xl_d[bass.ds(k, 1), :, :].rearrange("o p n -> p (o n)"),
                                     xl[:, r % 2, :]).then_inc(xl_stored[r % 2], 16)

                load(0, 0, 0)
                load(0, 0, 1)
                last = NBLK // UNROLL - 1
                for u in range(UNROLL):
                    iteration(0, u)
                with sp.Fori(1, last) as q:
                    for u in range(UNROLL):
                        iteration(q, u)
                for j in range(RBLK):
                    if j < 2:
                        sp.wait_ge(xl_stored[j], 16 * RBLK)
                    sp.dma_start(XL[0][:, WARM + j * BLOCK:WARM + (j + 1) * BLOCK],
                                 xl_d[j, :, :]).then_inc(region0_loaded, 16)
                for u in range(UNROLL + LAG):
                    iteration(last, u)
                for r in range(2):
                    sp.wait_ge(x1_stored[r], 16 * NBLK // 2)
                    sp.wait_ge(xl_stored[r], 16 * NBLK // 2)
                sp.wait_ge(region0_loaded, 16 * RBLK)

            @blk.tensor
            def _(pe):
                def center_x(q, u, s):
                    on, k, r = stage(q, u, 0)
                    if on:
                        if s == 0:
                            pe.wait_ge(x_loaded[r], 16 * (rounds(q, u, 0, 4) + 1))
                        g = 4 * k + s
                        if not isinstance(g, int) or g >= 2:
                            pe.wait_ge(normed[0], g - 1)
                        pe.matmul(psc[0][s % 2][:, :], center, xin[:, r, tile_cols(s)],
                                  start=True, stop=True).then_inc(centered[0], 1)

                def middle_tap(q, u, s):
                    on, k, r = stage(q, u, 1)
                    if on:
                        g = 4 * k + s
                        if s == 0:
                            pe.wait_ge(normed[0], 4 * k + 4)
                            if isinstance(k, int) and k == 0:
                                pe.wait_ge(pads_ready, 1)
                            else:
                                pe.wait_ge(halo_ready, 2 * k - 1)
                        if s == TPB - 1:
                            pe.wait_ge(halo_ready, 2 * k + 2)
                        if not isinstance(g, int) or g >= 1:
                            pe.wait_ge(acc_step, NACC * g - NACC + 1)
                        for n, t in enumerate(PE_TAPS):
                            i, j = t // 3, t % 3
                            m = pe.matmul(pst[:, :].rearrange("p (r w) -> p r w", w=W),
                                          taps[:, n * P:(n + 1) * P],
                                          xn[:, r % 2, RPT * s + i:RPT * s + i + RPT, j:j + W],
                                          start=(n == 0), stop=(n == len(PE_TAPS) - 1))
                        m.then_inc(taps_ready, 1)

                def center_x1(q, u, s):
                    on, k, r = stage(q, u, 2)
                    if on:
                        g = 4 * k + s
                        pe.wait_ge(x1_ready, g + 1)
                        if not isinstance(g, int) or g >= 2:
                            pe.wait_ge(normed[1], g - 1)
                        pe.matmul(psc[1][s % 2][:, :], center, x1[:, r % 2, tile_cols(s)],
                                  start=True, stop=True).then_inc(centered[1], 1)

                def var_x(q, u, s):
                    on, k, r = stage(q, u, 0)
                    if on:
                        g = 4 * k + s
                        pe.wait_ge(squared[0], g + 1)
                        if not isinstance(g, int) or g >= 1:
                            pe.wait_ge(ln_done[0], g)
                        pe.matmul(psv[0][:, :], meanm, sq[:, 0, :], start=True,
                                  stop=True).then_inc(var_ready[0], 1)

                def project(q, u, s):
                    on, k, r = stage(q, u, 3)
                    if on:
                        g = 4 * k + s
                        pe.wait_ge(normed[1], g + 1)
                        if not isinstance(g, int) or g >= 1:
                            pe.wait_ge(bn_done, g)
                        pe.matmul(psw[:, :], wT[:, :], xl[:, r % 2, tile_cols(s)],
                                  start=True, stop=True).then_inc(wx_ready, 1)

                def var_x1(q, u, s):
                    on, k, r = stage(q, u, 2)
                    if on:
                        g = 4 * k + s
                        pe.wait_ge(squared[1], g + 1)
                        if not isinstance(g, int) or g >= 1:
                            pe.wait_ge(ln_done[1], g)
                        pe.matmul(psv[1][:, :], meanm, sq[:, 1, :], start=True,
                                  stop=True).then_inc(var_ready[1], 1)

                def iteration(q, u):
                    for s in range(TPB):
                        center_x(q, u, s)
                        middle_tap(q, u, s)
                        center_x1(q, u, s)
                        var_x(q, u, s)
                        project(q, u, s)
                        var_x1(q, u, s)
                schedule(pe, iteration)

            @blk.scalar
            def _(act):
                act.preload_act_table_set("natural_log_exp_and_others")

                def square(q, u, s, l):
                    on, k, _ = stage(q, u, 2 * l)
                    if not on:
                        return
                    g = 4 * k + s
                    act.wait_ge(centered[l], g + 1)
                    if not isinstance(g, int) or g >= 1:
                        act.wait_ge(var_ready[l], g)
                    act.activation(sq[:, l, :], psc[l][s % 2][:, :], ACT.Square).then_inc(squared[l], 1)

                def rsqrt(q, u, s, l):
                    on, k, _ = stage(q, u, 2 * l)
                    if not on:
                        return
                    g = 4 * k + s
                    act.wait_ge(var_ready[l], g + 1)
                    if not isinstance(g, int) or g >= 1:
                        act.wait_ge(rstd_ready[l], g)
                    act.activation(ln[:, l, :], psv[l][:, :], ACT.Ln,
                                   bias=(eps_c, eps_t)[l]).then_inc(ln_done[l], 1)
                    act.wait_ge(ln_done[l], g + 1)
                    if not isinstance(g, int) or g >= 2:
                        act.wait_ge(normed[l], g - 1)
                    act.activation(rstd[:, l, s % 2, :], ln[:, l, :], ACT.Exp,
                                   scale=-0.5).then_inc(rstd_ready[l], 1)

                def first_row(q, u):
                    on, k, r = stage(q, u, 0)
                    if isinstance(k, int) and k == NBLK:
                        act.wait_ge(pads_ready, 2)
                        act.activation(xn[:, (r + 1) % 2, ROWS + 1, 1:W + 1], zero_row[:, :],
                                       ACT.Copy).then_inc(halo_ready, 1)
                    if on and (not isinstance(k, int) or k >= 1):
                        act.wait_ge(normed[0], 4 * k + 1)
                        act.activation(xn[:, (r + 1) % 2, ROWS + 1, 1:W + 1], xn[:, r % 2, 1, 1:W + 1],
                                       ACT.Copy).then_inc(halo_ready, 1)

                def last_row(q, u):
                    on, k, r = stage(q, u, 1)
                    if on:
                        act.wait_ge(normed[0], 4 * k + 4)
                        if not isinstance(k, int) or k >= 1:
                            act.wait_ge(acc_step, NACC * (4 * k - 3))
                        else:
                            act.wait_ge(pads_ready, 1)
                        act.activation(xn[:, (r + 1) % 2, 0, 1:W + 1], xn[:, r % 2, ROWS, 1:W + 1],
                                       ACT.Copy).then_inc(halo_ready, 1)

                def tap_product(q, u, s, n):
                    on, k, r = stage(q, u, 1)
                    if not on:
                        return
                    g = 4 * k + s
                    if n == 0 and s == 0:
                        act.wait_ge(normed[0], 4 * k + 4)
                        if isinstance(k, int) and k == 0:
                            act.wait_ge(pads_ready, 1)
                        else:
                            act.wait_ge(halo_ready, 2 * k - 1)
                    if n == 0 and s == TPB - 1:
                        act.wait_ge(halo_ready, 2 * k + 2)
                    if not isinstance(g, int) or g >= 1:
                        act.wait_ge(product_added, NPROD * (g - 1) + n + 1)
                    i, j = ACT_TAPS[n] // 3, ACT_TAPS[n] % 3
                    act.activation(prod[:, n, :, :], xn[:, r % 2, RPT * s + i:RPT * s + i + RPT, j:j + W],
                                   ACT.Copy, scale=kk[:, ACT_TAPS[n]:ACT_TAPS[n] + 1]).then_inc(products, 1)

                def iteration(q, u):
                    for s in range(TPB):
                        if s == 1:
                            first_row(q, u)
                        square(q, u, s, 0)
                        tap_product(q, u, s, 0)
                        if s == 0:
                            last_row(q, u)
                        tap_product(q, u, s, 1)
                        square(q, u, s, 1)
                        rsqrt(q, u, s, 0)
                        tap_product(q, u, s, 2)
                        rsqrt(q, u, s, 1)
                schedule(act, iteration)

            @blk.gpsimd
            def _(pool):
                pool.memset(xn[:, :, :, :].rearrange("p a r w -> p (a r w)"), 0.0).then_inc(pads_ready, 1)
                pool.wait_ge(pads_ready, 1)
                pool.memset(zero_row[:, :], 0.0).then_inc(pads_ready, 1)

                def finish(q, u, lag, s):
                    on, k, r = stage(q, u, lag)
                    if not on:
                        return
                    g = 4 * k + s
                    pool.wait_ge(product_added, NPROD * g + NPROD)
                    pool.wait_ge(acc_step, NACC * g + NACC)
                    if s == 0 and (not isinstance(k, int) or k >= 2):
                        pool.wait_ge(centered[1], 4 * k - 4)
                        pool.wait_ge(x1_stored[r % 2], 16 * rounds(q, u, lag, 2))
                    pool.tensor_tensor(x1[:, r % 2, tile_cols(s)],
                                       acc[:, s % 2, :, :].rearrange("p r w -> p (r w)"),
                                       xr[:, s % 2, :], ALU.add).then_inc(x1_ready, 1)

                def add_product(q, u, s, n):
                    on, k, r = stage(q, u, 1)
                    if not on:
                        return
                    g = 4 * k + s
                    if n == 0 and (not isinstance(g, int) or g >= 2):
                        pool.wait_ge(x1_ready, g - 1)
                    pool.wait_ge(products, NPROD * g + n + 1)
                    if n:
                        pool.wait_ge(product_added, NPROD * g + n)
                    pool.tensor_tensor(xr[:, s % 2, :], prod[:, n, :, :].rearrange("p r w -> p (r w)"),
                                       xr[:, s % 2, :] if n else xin[:, r, tile_cols(s)],
                                       ALU.add).then_inc(product_added, 1)

                def iteration(q, u):
                    for s in range(TPB):
                        add_product(q, u, s, 0)
                        if s:
                            finish(q, u, 1, s - 1)
                        else:
                            finish(q, u, 2, TPB - 1)
                        for n in range(1, NPROD):
                            add_product(q, u, s, n)
                schedule(pool, iteration)

            @blk.vector
            def _(dve):
                dve.wait_ge(pads_ready, 1)

                def norm_x(q, u, s):
                    on, k, r = stage(q, u, 0)
                    if on:
                        g = 4 * k + s
                        if s == 0 and (not isinstance(k, int) or k >= 2):
                            dve.wait_ge(products, NPROD * (4 * k - 4))
                            dve.wait_ge(acc_step, NACC * (4 * k - 4))
                            dve.wait_ge(halo_ready, 2 * k - 3)
                        dve.wait_ge(rstd_ready[0], g + 1)
                        dve.tensor_tensor(xn[:, r % 2, 1 + RPT * s:1 + RPT * (s + 1), 1:W + 1],
                                          psc[0][s % 2][:, :].rearrange("p (r w) -> p r w", w=W),
                                          rstd[:, 0, s % 2, :].rearrange("p (r w) -> p r w", w=W),
                                          ALU.mult).then_inc(normed[0], 1)

                def tap(q, u, s, n):
                    on, k, r = stage(q, u, 1)
                    if not on:
                        return
                    g = 4 * k + s
                    if n == 0:
                        if s == 0:
                            dve.wait_ge(normed[0], 4 * k + 4)
                            if isinstance(k, int) and k == 0:
                                dve.wait_ge(pads_ready, 1)
                            else:
                                dve.wait_ge(halo_ready, 2 * k - 1)
                        if s == TPB - 1:
                            dve.wait_ge(halo_ready, 2 * k + 2)
                        dve.wait_ge(taps_ready, g + 1)
                        if not isinstance(g, int) or g >= 2:
                            dve.wait_ge(x1_ready, g - 1)
                    i, j = DVE_TAPS[n] // 3, DVE_TAPS[n] % 3
                    if n:
                        dve.wait_ge(acc_step, NACC * g + n)
                        prev = acc[:, s % 2, :, :]
                    else:
                        prev = pst[:, :].rearrange("p (r w) -> p r w", w=W)
                    dve.scalar_tensor_tensor(
                        out=acc[:, s % 2, :, :],
                        in0=xn[:, r % 2, RPT * s + i:RPT * s + i + RPT, j:j + W],
                        scalar=kk[:, DVE_TAPS[n]:DVE_TAPS[n] + 1], in1=prev, op0=ALU.mult,
                        op1=ALU.add).then_inc(acc_step, 1)

                def statistics(q, u, s):
                    on, k, r = stage(q, u, 3)
                    if on:
                        g = 4 * k + s
                        dve.wait_ge(wx_ready, g + 1)
                        dve.bn_stats(stats[:, bass.ds(g, 1), :].rearrange("p o n -> p (o n)"),
                                     psw[:, :]).then_inc(bn_done, 1)

                def norm_x1(q, u, s):
                    on, k, r = stage(q, u, 2)
                    if on:
                        g = 4 * k + s
                        if s == 0 and (not isinstance(k, int) or k >= 2):
                            dve.wait_ge(wx_ready, 4 * k - 4)
                            dve.wait_ge(xl_stored[r % 2], 16 * rounds(q, u, 2, 2))
                        dve.wait_ge(rstd_ready[1], g + 1)
                        dve.tensor_tensor(xl[:, r % 2, tile_cols(s)], psc[1][s % 2][:, :],
                                          rstd[:, 1, s % 2, :], ALU.mult).then_inc(normed[1], 1)

                def iteration(q, u):
                    for s in range(TPB):
                        tap(q, u, s, 0)
                        statistics(q, u, s)
                        norm_x(q, u, s)
                        tap(q, u, s, 1)
                        tap(q, u, s, 2)
                        norm_x1(q, u, s)
                        tap(q, u, s, 3)
                        tap(q, u, s, 4)
                schedule(dve, iteration)

        with ExitStack() as ph:
            wps = ph.enter_context(nc.psum_tensor("wps", [P, P], F32))
            bps = ph.enter_context(nc.psum_tensor("bps", [P, 2], F32))
            step, mm = sem("bn_step", ph), sem("bn_mm", ph)
            rs = sem("bn_rs", ph)
            blk = ph.enter_context(nc.Block())

            @blk.vector
            def _(dve):
                dve.bn_aggr(bn[:, 0:2], stats[:, :, :].rearrange("p t n -> p (t n)")).then_inc(step, 1)
                dve.wait_ge(mm, 1)
                dve.tensor_copy(bn[:, 2:3], bps[:, 0:1]).then_inc(step, 1)
                dve.wait_ge(step, 2)
                dve.tensor_tensor(bn[:, 3:4], bn[:, 0:1], bn[:, 2:3], ALU.subtract).then_inc(step, 1)
                dve.wait_ge(step, 3)
                dve.scalar_tensor_tensor(out=bn[:, 4:5], in0=bn[:, 3:4], scalar=bn[:, 3:4],
                                         in1=bn[:, 1:2], op0=ALU.mult, op1=ALU.add).then_inc(step, 1)
                dve.wait_ge(rs, 2)
                dve.tensor_tensor(bn[:, 6:7], bn[:, 3:4], gam, ALU.mult).then_inc(step, 1)
                dve.wait_ge(step, 5)
                dve.tensor_tensor(bn[:, 4:5], bn[:, 2:3], bn[:, 6:7], ALU.mult).then_inc(step, 1)
                dve.wait_ge(step, 6)
                dve.tensor_tensor(bn[:, 7:8], bet, bn[:, 4:5], ALU.subtract).then_inc(step, 1)
                dve.tensor_scalar(w_rows[:, :], w_rows[:, :], bn[:, 6:7], None, ALU.mult).then_inc(step, 1)
                dve.wait_ge(mm, 3)
                dve.tensor_copy(wT[:, :], wps[:, :]).then_inc(step, 1)

            @blk.tensor
            def _(pe):
                pe.wait_ge(step, 1)
                pe.matmul(bps[:, 0:1], pairm, bn[:, 0:1], start=True, stop=True).then_inc(mm, 1)
                pe.wait_ge(step, 4)
                pe.matmul(bps[:, 1:2], pairm, bn[:, 4:5], start=True, stop=True).then_inc(mm, 1)
                pe.wait_ge(step, 8)
                pe.transpose(wps[:, :], w_rows[:, :], ident).then_inc(mm, 1)

            @blk.scalar
            def _(act):
                act.preload_act_table_set("natural_log_exp_and_others")
                act.wait_ge(mm, 2)
                act.activation(bn[:, 5:6], bps[:, 1:2], ACT.Ln, bias=eps_t).then_inc(rs, 1)
                act.wait_ge(rs, 1)
                act.activation(bn[:, 3:4], bn[:, 5:6], ACT.Exp, scale=-0.5).then_inc(rs, 1)

        bias_w = bn[:, 7:8]
        keys = ExitStack()
        stack.enter_context(keys)
        xsub = sb("xsub", [P, NSUB], F32, keys)
        flag = sb("flag", [P, 1], I32, keys)
        last_stored = sem("last_stored", keys)

        def take_keys(pool, block, src_rows):
            v = src_rows.rearrange("p (r w) -> p r w", w=W)
            return pool.tensor_copy(
                xsub[:, bass.ds(block * SUBB, SUBB)].rearrange("p (r w) -> p r w", w=W // SUB),
                v[:, SUB0:ROWS:SUB, SUB0:W:SUB])

        with ExitStack() as ph:
            XL.append(sb("region1", [P, WARM + RLEN], F32, ph))
            ws = sb("warm_state", [P, 2, CHUNKS], F32, ph)
            reached = sb("reached", [P, CHUNKS], F32, ph)
            true = sb("true_state", [P, 1 + CHUNKS], F32, ph)
            diff = sb("diff", [P, CHUNKS], F32, ph)
            dmax = sb("dmax", [P, REGIONS + 1], F32, ph)
            dall = sb("dall", [1, P + 2], F32, ph)
            xb = sb("x1_block", [P, 3, BLOCK], F32, ph)
            HALF = CHUNKS // 2
            pss = [[ph.enter_context(nc.psum_tensor(f"pss{j}{h}", [P, HALF], F32)) for h in range(2)] for j in range(2)]
            pdm = ph.enter_context(nc.psum_tensor("pdm", [1, P], F32))
            S = lambda n: sem(n, ph)
            warm_loaded = [S(f"warm_loaded{j}") for j in range(2)]
            region_loaded = [S(f"region_loaded{j}") for j in range(2)]
            x1_loaded = [S(f"x1_loaded{j}") for j in range(3)]
            x2_stored = [S(f"x2_stored{j}") for j in range(3)]
            sums_ready = [S(f"sums_ready{h}") for h in range(2)]
            y_ready = [S(f"y_ready{h}") for h in range(2)]
            fixed = S("fixed")
            kept = S("states_kept")
            added = S("added")
            key_taken = S("key_taken")
            checked = S("checked")
            dstep = S("dstep")
            dmm = S("dmm")
            zero_warm = S("zero_warm")
            last_x1_loaded = S("last_x1_loaded")
            blk = ph.enter_context(nc.Block())
            UN = 4
            last_warm = (WARM - 1) % 2

            LAST = NBLK - RBLK

            def last_x1(j):
                return XL[REGIONS % 2][:, WARM + j * BLOCK:WARM + (j + 1) * BLOCK]

            def at(buf, n, h):
                return XL[buf][:, bass.ds(n + h * HALF * CLEN, HALF, step=CLEN)]

            def ws_at(n, h):
                return ws[:, n % 2, h * HALF:(h + 1) * HALF]

            def wait_y(eng, n):
                for h in range(2):
                    eng.wait_ge(y_ready[h], n)

            @blk.sync
            def _(sp):
                def load_region(r):
                    b = r % 2
                    if r >= 2:
                        sp.wait_ge(added, RBLK * (r - 1))
                        sp.wait_ge(kept, 2 * (r - 1))
                    if r:
                        sp.dma_start(XL[b][:, 0:WARM],
                                     xl_d[r * RBLK - 1, :, BLOCK - WARM:BLOCK]).then_inc(warm_loaded[b], 16)
                    for j in range(RBLK):
                        sp.dma_start(XL[b][:, WARM + j * BLOCK:WARM + (j + 1) * BLOCK],
                                     xl_d[r * RBLK + j, :, :]).then_inc(region_loaded[b], 16)

                def store(k):
                    sp.wait_ge(added, k + 1)
                    sp.dma_start(x2_d[k, :, :], xb[:, k % 3, :]).then_inc(x2_stored[k % 3], 16)

                load_region(1)
                for k in range(LAST):
                    slot = k % 3
                    if k >= 3:
                        sp.wait_ge(x2_stored[slot], 16 * (k // 3))
                        sp.wait_ge(key_taken, k - 2)
                    sp.dma_start(xb[:, slot, :], x1_d[k, :, :]).then_inc(x1_loaded[slot], 16)
                    if k >= 1:
                        store(k - 1)
                    if k % RBLK == 0 and 1 <= k // RBLK < REGIONS - 1:
                        load_region(k // RBLK + 1)
                store(LAST - 1)
                sp.wait_ge(added, LAST)
                sp.wait_ge(kept, 2 * (REGIONS - 1))
                for j in range(RBLK):
                    sp.dma_start(last_x1(j), x1_d[LAST + j, :, :]).then_inc(last_x1_loaded, 16)
                for j in range(RBLK):
                    sp.wait_ge(added, LAST + j + 1)
                    sp.dma_start(x2_d[LAST + j, :, :], last_x1(j)).then_inc(last_stored, 16)
                for slot in range(3):
                    sp.wait_ge(x2_stored[slot], 16 * len(range(slot, LAST, 3)))

            @blk.tensor
            def _(pe):
                def step(n, par, h, before, after):
                    pe.matmul(pss[par][h][:, :], wT[:, :], at(b, n, h), start=True, stop=False)
                    pe.wait_ge(y_ready[h], after)
                    pe.matmul(pss[par][h][:, :], vT[:, :], before, start=False,
                              stop=True).then_inc(sums_ready[h], 1)

                for r in range(REGIONS):
                    b, base = r % 2, r * STEPS
                    if r == 0:
                        pe.wait_ge(zero_warm, 1)
                    else:
                        pe.wait_ge(warm_loaded[b], 16 * ((r + 1) // 2))
                        pe.wait_ge(region_loaded[b], 16 * RBLK * ((r + 1) // 2))
                        wait_y(pe, base)
                    for h in range(2):
                        pe.matmul(pss[0][h][:, :], wT[:, :], at(b, 0, h), start=True,
                                  stop=True).then_inc(sums_ready[h], 1)
                    for n in range(1, WARM + 1):
                        for h in range(2):
                            if n == WARM and r == 0 and h == 0:
                                pe.wait_ge(fixed, 1)
                            step(n, n % 2, h, ws_at(n - 1, h), base + n)
                    for v in range(1, UN):
                        for h in range(2):
                            step(WARM + v, v % 2, h, at(b, WARM + v - 1, h), base + WARM + v)
                    with pe.Fori(1, CLEN // UN) as t:
                        for v in range(UN):
                            for h in range(2):
                                step(t * UN + (WARM + v), v % 2, h, at(b, t * UN + (WARM + v - 1), h),
                                     t * UN + (base + WARM + v))
                pe.wait_ge(checked, REGIONS)
                pe.transpose(pdm[0:1, :], dmax[:, REGIONS:REGIONS + 1], ident).then_inc(dmm, 1)

            @blk.scalar
            def _(act):
                act.preload_act_table(ACT.Sigmoid)
                for r in range(REGIONS):
                    b, base = r % 2, r * STEPS
                    for n in range(WARM):
                        for h in range(2):
                            act.wait_ge(sums_ready[h], base + n + 1)
                            if n == last_warm and r:
                                act.wait_ge(kept, 2 * r - 1)
                            act.activation(ws_at(n, h), pss[n % 2][h][:, :], ACT.Sigmoid,
                                           bias=bias_w).then_inc(y_ready[h], 1)
                    if r == 0:
                        act.wait_ge(y_ready[0], WARM)
                        act.activation(ws[:, last_warm, 0:1], ws[:, last_warm, 0:1], ACT.Copy,
                                       scale=0.0).then_inc(fixed, 1)

                    with act.Fori(0, CLEN // UN) as t:
                        for v in range(UN):
                            for h in range(2):
                                act.wait_ge(sums_ready[h], t * UN + (base + WARM + v + 1))
                                act.activation(at(b, t * UN + (WARM + v), h), pss[v % 2][h][:, :], ACT.Sigmoid,
                                               bias=bias_w).then_inc(y_ready[h], 1)

            @blk.gpsimd
            def _(pool):
                pool.memset(XL[0][:, 0:WARM], 0.0).then_inc(zero_warm, 1)
                pool.memset(true[:, 0:1], 0.0).then_inc(zero_warm, 1)
                for r in range(REGIONS):
                    b = r % 2
                    wait_y(pool, r * STEPS + WARM)
                    if r == 0:
                        pool.wait_ge(fixed, 1)
                    else:
                        pool.wait_ge(checked, r)
                    pool.tensor_copy(reached[:, :], ws[:, last_warm, :]).then_inc(kept, 1)
                    wait_y(pool, (r + 1) * STEPS)
                    pool.tensor_copy(true[:, 1:1 + CHUNKS],
                                     XL[b][:, WARM + CLEN - 1:WARM + RLEN:CLEN]).then_inc(kept, 1)
                    for j in range(RBLK):
                        k = r * RBLK + j
                        pool.wait_ge(added, k + 1)
                        take_keys(pool, k, xb[:, k % 3, :] if k < LAST else last_x1(j)).then_inc(key_taken, 1)

            @blk.vector
            def _(dve):
                n = 0
                dve.wait_ge(zero_warm, 2)
                for r in range(REGIONS):
                    dve.wait_ge(kept, 2 * r + 2)
                    dve.tensor_tensor(diff[:, :], reached[:, :], true[:, 0:CHUNKS],
                                      ALU.subtract).then_inc(dstep, 1)
                    n += 1
                    dve.wait_ge(dstep, n)
                    dve.tensor_reduce(dmax[:, r:r + 1], diff[:, :], AX.X, ALU.max,
                                      apply_absolute_value=True).then_inc(dstep, 1)
                    dve.tensor_copy(true[:, 0:1], true[:, CHUNKS:CHUNKS + 1]).then_inc(dstep, 1)
                    n += 2
                    dve.wait_ge(dstep, n)
                    if r == REGIONS - 1:
                        dve.tensor_reduce(dmax[:, REGIONS:REGIONS + 1], dmax[:, 0:REGIONS], AX.X,
                                          ALU.max).then_inc(checked, 1)
                    else:
                        dve.sem_inc(checked, 1)
                    wait_y(dve, (r + 1) * STEPS)
                    for j in range(RBLK):
                        k = r * RBLK + j
                        if k < LAST:
                            x1_x2 = xb[:, k % 3, :]
                            dve.wait_ge(x1_loaded[k % 3], 16 * (k // 3 + 1))
                        else:
                            x1_x2 = last_x1(j)
                            dve.wait_ge(last_x1_loaded, 16 * RBLK)
                        dve.tensor_tensor(x1_x2, x1_x2,
                                          XL[r % 2][:, WARM + j * BLOCK:WARM + (j + 1) * BLOCK],
                                          ALU.add).then_inc(added, 1)
                dve.wait_ge(dmm, 1)
                dve.tensor_copy(dall[0:1, 0:P], pdm[0:1, :]).then_inc(dstep, 1)
                dve.wait_ge(dstep, n + 1)
                dve.tensor_reduce(dall[0:1, P:P + 1], dall[0:1, 0:P], AX.X, ALU.max).then_inc(dstep, 1)
                dve.wait_ge(dstep, n + 2)
                dve.tensor_scalar(flag[0:1, :], dall[0:1, P:P + 1], STATE_TOL, None,
                                  ALU.is_le).then_inc(dstep, 1)

        with ExitStack() as ph:
            xs = sb("seq_xl", [P, BLOCK], F32, ph)
            ys = sb("seq_y", [P, 1 + BLOCK], F32, ph)
            xr = sb("seq_x", [P, BLOCK], F32, ph)
            pq = ph.enter_context(nc.psum_tensor("pq", [P, 1], F32))
            S = lambda n: sem(n, ph)
            seq_loaded, seq_sums, seq_y = S("seq_loaded"), S("seq_sums"), S("seq_y_ready")
            seq_added, seq_carried, seq_stored, seq_keys = S("seq_added"), S("seq_carried"), S("seq_stored"), S("seq_keys")
            blk = ph.enter_context(nc.Block())

            def unreached(eng):
                return eng.value_load(flag[0:1, 0:1], min_val=0, max_val=1) == 0

            @blk.sync
            def _(sp):
                with sp.If(unreached(sp)):
                    sp.wait_ge(last_stored, 16 * RBLK)
                    with sp.Fori(0, NBLK) as k:
                        sp.wait_ge(seq_added, k + 1)
                        sp.sem_inc(held, 1)
                        sp.wait_ge(seq_keys, k + 1)
                        sp.sem_inc(held, 1)
                        sp.wait_ge(seq_stored, k * 16 + 16)
                        sp.dma_start(xs[:, :], xl_d[bass.ds(k, 1), :, :].rearrange("o p n -> p (o n)")).then_inc(seq_loaded, 16)
                        sp.dma_start(xr[:, :], x1_d[bass.ds(k, 1), :, :].rearrange("o p n -> p (o n)")).then_inc(seq_loaded, 16)
                        sp.wait_ge(seq_added, k + 2)
                        sp.sem_inc(held, 1)
                        sp.dma_start(x2_d[bass.ds(k, 1), :, :].rearrange("o p n -> p (o n)"), xr[:, :]).then_inc(seq_stored, 16)
                    sp.wait_ge(seq_stored, 16 * NBLK + 16)

            @blk.tensor
            def _(pe):
                with pe.If(unreached(pe)):
                    with pe.Fori(0, NBLK) as k:
                        pe.wait_ge(seq_loaded, k * 32 + 32)
                        pe.wait_ge(seq_carried, k + 1)
                        pe.sem_inc(held, 1)
                        with pe.Fori(0, BLOCK) as t:
                            pe.wait_ge(seq_y, k * BLOCK + t + 1)
                            pe.matmul(pq[:, :], wT[:, :], xs[:, bass.ds(t, 1)], start=True, stop=False)
                            pe.matmul(pq[:, :], vT[:, :], ys[:, bass.ds(t, 1)], start=False,
                                      stop=True).then_inc(seq_sums, 1)

            @blk.scalar
            def _(act):
                act.preload_act_table(ACT.Sigmoid)
                with act.If(unreached(act)):
                    with act.Fori(0, NBLK) as k:
                        act.wait_ge(seq_added, k + 1)
                        act.wait_ge(seq_carried, k + 1)
                        with act.Fori(0, BLOCK) as t:
                            act.wait_ge(seq_sums, k * BLOCK + t + 1)
                            act.activation(ys[:, bass.ds(t + 1, 1)], pq[:, :], ACT.Sigmoid,
                                           bias=bias_w).then_inc(seq_y, 1)

            @blk.vector
            def _(dve):
                with dve.If(unreached(dve)):
                    for ahead, n in ((seq_y, 1), (seq_added, 1), (seq_keys, 1), (seq_stored, 16)):
                        dve.sem_inc(ahead, n)
                    dve.memset(ys[:, 0:1], 0.0).then_inc(seq_carried, 1)
                    with dve.Fori(0, NBLK) as k:
                        dve.wait_ge(seq_loaded, k * 32 + 32)
                        dve.wait_ge(seq_y, k * BLOCK + BLOCK + 1)
                        dve.tensor_tensor(xr[:, :], xr[:, :], ys[:, 1:1 + BLOCK], ALU.add).then_inc(seq_added, 1)
                        dve.tensor_copy(ys[:, 0:1], ys[:, BLOCK:BLOCK + 1]).then_inc(seq_carried, 1)

            @blk.gpsimd
            def _(pool):
                with pool.If(unreached(pool)):
                    with pool.Fori(0, NBLK) as k:
                        pool.wait_ge(seq_added, k + 2)
                        take_keys(pool, k, xr[:, :]).then_inc(seq_keys, 1)

        with ExitStack() as ph:
            RING = 3
            sqk = sb("sqk", [P, 2, TILE], F32, ph)
            lnk = sb("lnk", [P, TILE], F32, ph)
            rsk = sb("rsk", [P, 2, TILE], F32, ph)
            t_kv = sb("t_kv", [P, RING, 2, 2 * P], F32, ph)
            ek = sb("ek", [P, RING, 2, P], F32, ph)
            gm = sb("gm", [P, P], F32, ph)
            psa = [ph.enter_context(nc.psum_tensor(f"psa{j}", [P, TILE], F32)) for j in range(3)]
            psb = ph.enter_context(nc.psum_tensor("psb", [P, TILE], F32))
            pkv = [ph.enter_context(nc.psum_tensor(f"pkv{j}", [P, 2, 2 * P], F32)) for j in range(2)]
            pg = ph.enter_context(nc.psum_tensor("pg", [P, P], F32))
            psum_k = ph.enter_context(nc.psum_tensor("psum_k", [P, 1], F32))
            pm = psb[:, 0:P]
            S = lambda n: sem(n, ph)
            kc, ksq, kv_, kln, krs, kn = (S(n) for n in ("k_centered", "k_squared", "k_var", "k_ln", "k_rstd", "k_normed"))
            kvp, kvb_done, kexp, kmap, kvacc, kst, kmm, krelu = (S(n) for n in ("kv_product", "kv_biased", "k_exp", "k_mapped", "kv_summed", "k_step", "k_mm", "k_relu"))
            blk = ph.enter_context(nc.Block())
            KT = NSUB // TILE
            NPAIR = NSUB // P // 2

            @blk.sync
            def _(sp):
                sp.wait_ge(last_stored, 16 * RBLK)

            @blk.tensor
            def _(pe):
                for t in range(KT + 1):
                    if t < KT:
                        if t >= 3:
                            pe.wait_ge(kn, t - 2)
                        pe.matmul(psa[t % 3][:, :], center, xsub[:, t * TILE:(t + 1) * TILE], start=True, stop=True).then_inc(kc, 1)
                    if t:
                        pe.wait_ge(ksq, t)
                        if t >= 2:
                            pe.wait_ge(kln, t - 1)
                        pe.matmul(psb[:, :], meanm, sqk[:, (t - 1) % 2, :], start=True, stop=True).then_inc(kv_, 1)
                for c in range(NPAIR + RING - 1):
                    if c < NPAIR:
                        if c % (TILE // P // 2) == 0:
                            pe.wait_ge(kn, c // (TILE // P // 2) + 1)
                        if c >= 2:
                            pe.wait_ge(kvb_done, c - 1)
                        for i in range(2):
                            m = pe.matmul(pkv[c % 2][:, i, :], xsub[:, (2 * c + i) * P:(2 * c + i + 1) * P], kvT[:, :],
                                          start=True, stop=True)
                        m.then_inc(kvp, 1)
                    d = c - (RING - 1)
                    if d >= 0:
                        pe.wait_ge(kmap, d + 1)
                        for i in range(2):
                            first, last = d == 0 and i == 0, d == NPAIR - 1 and i == 1
                            pe.matmul(pg[:, :], t_kv[:, d % RING, i, P:2 * P], t_kv[:, d % RING, i, 0:P], start=first,
                                      stop=last)
                            m = pe.matmul(psum_k[:, :], t_kv[:, d % RING, i, 0:P], ones[:, :], start=first, stop=last)
                        m.then_inc(kvacc, 1)
                pe.wait_ge(kst, 1)
                pe.matmul(pm, gm[:, :], pT[:, :], start=True, stop=True).then_inc(kmm, 1)

            @blk.scalar
            def _(act):
                act.preload_act_table_set("natural_log_exp_and_others")
                for t in range(KT + 1):
                    if t < KT:
                        act.wait_ge(kc, t + 1)
                        if t >= 2:
                            act.wait_ge(kv_, t - 1)
                        act.activation(sqk[:, t % 2, :], psa[t % 3][:, :], ACT.Square).then_inc(ksq, 1)
                    if t:
                        act.wait_ge(kv_, t)
                        if t >= 2:
                            act.wait_ge(krs, t - 1)
                        act.activation(lnk[:, :], psb[:, :], ACT.Ln, bias=eps_c).then_inc(kln, 1)
                        act.wait_ge(kln, t)
                        if t >= 3:
                            act.wait_ge(kn, t - 2)
                        act.activation(rsk[:, (t - 1) % 2, :], lnk[:, :], ACT.Exp, scale=-0.5).then_inc(krs, 1)
                for c in range(NPAIR):
                    act.wait_ge(kvb_done, c + 1)
                    if c >= RING:
                        act.wait_ge(kmap, c - RING + 1)
                    act.activation(ek[:, c % RING, :, :], t_kv[:, c % RING, :, 0:P], ACT.Exp).then_inc(kexp, 1)

            @blk.vector
            def _(dve):
                for t in range(KT):
                    dve.wait_ge(krs, t + 1)
                    dve.tensor_tensor(xsub[:, t * TILE:(t + 1) * TILE], psa[t % 3][:, :], rsk[:, t % 2, :], ALU.mult).then_inc(kn, 1)
                for c in range(NPAIR + 1):
                    if c < NPAIR:
                        dve.wait_ge(kvp, c + 1)
                        if c >= RING:
                            dve.wait_ge(kvacc, c - RING + 1)
                        dve.tensor_tensor(t_kv[:, c % RING, :, :], pkv[c % 2][:, :, :],
                                          kvb[:, :].unsqueeze(1).to_broadcast([P, 2, 2 * P]), ALU.add).then_inc(kvb_done, 1)
                    if c:
                        k = t_kv[:, (c - 1) % RING, :, 0:P]
                        dve.wait_ge(kexp, c)
                        dve.tensor_scalar(k, k, 0.0, None, ALU.max).then_inc(krelu, 1)
                        dve.wait_ge(krelu, c)
                        dve.scalar_tensor_tensor(out=k, in0=ek[:, (c - 1) % RING, :, :], scalar=1.0,
                                                 in1=k, op0=ALU.min, op1=ALU.add).then_inc(kmap, 1)
                dve.wait_ge(kvacc, NPAIR)
                dve.tensor_tensor(gm[:, :], pg[:, :], headm, ALU.mult).then_inc(kst, 1)
                dve.tensor_scalar(dT[:, :], headm, psum_k[:, 0:1], None, ALU.mult).then_inc(kst, 1)
                dve.wait_ge(kmm, 1)
                dve.tensor_copy(mT[:, :], pm).then_inc(kst, 1)

        keys.close()
        regions.close()

        tail = ExitStack()
        stack.enter_context(tail)
        w1_sb = sb("w1_sb", [P, E // 2, HID], F32, tail)
        w1b_sb = sb("w1b_sb", [E, HID], F32, tail)
        w2_sb = sb("w2_sb", [P, 2, E, C], F32, tail)
        w2b_sb = sb("w2b_sb", [E, C], F32, tail)
        cand = sb("cand", [P, NBLK * K], F32, tail)
        cidx = sb("cidx", [P, NBLK * K], F32, tail)
        ses = sb("ses", [P, NBLK], F32, tail)
        with ExitStack() as ph:
            xb = sb("x2_block", [P, 4, BLOCK], F32, ph)
            x3 = sb("x3_block", [P, 2, BLOCK], F32, ph)
            sq = sb("sq3", [P, TILE], F32, ph)
            sq4 = sb("sq4", [P, 2, TILE], F32, ph)
            mean_sq = sb("mean_sq", [P, 2, TILE], F32, ph)
            var4 = sb("var4", [P, TILE], F32, ph)
            ln = sb("ln3", [P, 2, TILE], F32, ph)
            rstd = sb("rstd3", [P, 2, 2, TILE], F32, ph)
            xn = sb("xn3", [P, 2, TILE], F32, ph)
            eq = sb("exp_q", [P, 2, TILE], F32, ph)
            rq = sb("relu_q", [P, 2, TILE], F32, ph)
            qm = sb("q_map", [P, 2, TILE], F32, ph)
            lnd = sb("ln_d", [P, TILE], F32, ph)
            zr = sb("z_inv", [P, 2, TILE], F32, ph)
            qz = sb("q_z", [P, 2, TILE], F32, ph)
            xt = sb("x3_squares", [P, 2, BLOCK], F32, ph)
            lg = sb("logits", [P, 2, BLOCK // 2], F32, ph)
            eg = sb("exp_logits", [P, BLOCK // 2], F32, ph)
            m8 = sb("best8", [P, 2, K], F32, ph)
            i8 = sb("best8_at", [P, 2, K], U32, ph)
            nm = sb("neg_best", [P, 2, 1], F32, ph)
            se = sb("sum_exp", [P, 2, 1], F32, ph)
            pa3, pv3, pq, pd, pm3, pxe, pxo, pe2 = (
                ph.enter_context(nc.psum_tensor(n, [P, TILE], F32))
                for n in ("pa3", "pv3", "pq3", "pd3", "pm3", "gate_even", "gate_odd", "second_moment"))
            px = (pxe, pxo)
            S = lambda n: sem(n, ph)
            x2_loaded = [S(f"x2_loaded{r}") for r in range(4)]
            x3_stored = [S(f"x3_stored{r}") for r in range(2)]
            xt_stored = [S(f"xt_stored{r}") for r in range(2)]
            turned = S("turned")
            w_loaded = S("expert_weights_loaded")
            centered, squared, var_ready = S("centered3"), S("squared3"), S("var_ready3")
            ln_done, rstd_ready, normed = S("ln_done3"), S("rstd_ready3"), S("normed3")
            projected, squared4, moment_ready, mean_squared, scaled = (
                S(n) for n in ("projected", "squared4", "moment_ready", "mean_squared", "scaled"))
            var4_ready, clamped, ln4_done, rstd4_ready, biased = (
                S(n) for n in ("var4_ready", "clamped", "ln4_done", "rstd4_ready", "biased"))
            q_ready, expq_ready, relu_ready, mapped = S("q_ready"), S("expq_ready"), S("relu_ready"), S("mapped")
            d_ready, lnd_done, z_ready, qz_ready = S("d_ready"), S("lnd_done"), S("z_ready"), S("qz_ready")
            m_ready, x3_ready = S("m_ready"), S("x3_ready")
            best_ready, at_ready, neg_ready, expsum_ready, gathered = S("best_ready"), S("at_ready"), S("neg_ready"), S("expsum_ready"), S("gathered")
            blk = ph.enter_context(nc.Block())
            NSLOT = UNROLL * TPB
            LAG = 8

            def schedule(eng, slot):
                for m in range(NSLOT):
                    slot(0, m)
                with eng.Fori(1, NT // NSLOT) as q:
                    for m in range(NSLOT):
                        slot(q, m)
                for m in range(LAG + 1):
                    slot(NT // NSLOT, m)

            def stage(q, m, lag):
                t = NSLOT * q + (m - lag)
                active = not isinstance(t, int) or 0 <= t < NT
                return active, t, (m - lag) // TPB % UNROLL, (m - lag) % TPB

            def pair_of(q, m, lag):
                half = slice((m - lag) % 2 * 64, (m - lag) % 2 * 64 + 64)
                return NSLOT // 2 * q + (m - lag) // 2, (m - lag) // 2 % 2, half

            def past(t, n):
                return not isinstance(t, int) or t >= n

            def cols_of(s):
                return slice(s * TILE, (s + 1) * TILE)

            @blk.sync
            def _(sp):
                def load(k, r):
                    sp.dma_start(xb[:, r, :], x2_d[bass.ds(k, 1), :, :].rearrange("o p n -> p (o n)")).then_inc(x2_loaded[r], 16)

                def store(k, r):
                    sp.wait_ge(x3_ready, 4 * k + 4)
                    sp.dma_start(out_v[:, bass.ds(k * BLOCK, BLOCK)], x3[:, r % 2, :]).then_inc(x3_stored[r % 2], 16)
                    sp.wait_ge(turned, 4 * k + 4)
                    sp.dma_start(xt_d[k, :, :], xt[:, r % 2, :]).then_inc(xt_stored[r % 2], 16)

                for k in range(3):
                    load(k, k)
                for j in range(2):
                    sp.dma_start(w1_sb[j * C:(j + 1) * C, :, :],
                                 w1[j::2, 0:C, :].rearrange("e d h -> d e h")).then_inc(w_loaded, 16)
                sp.dma_start(w1b_sb[:, :], w1[:, C, :]).then_inc(w_loaded, 16)
                for j in range(2):
                    sp.dma_start(w2_sb[:, j, :, :], w2[:, j * P:(j + 1) * P, :].rearrange("e p o -> p e o")).then_inc(w_loaded, 16)
                sp.dma_start(w2b_sb[:, :], w2[:, HID, :]).then_inc(w_loaded, 16)
                for k in range(NBLK):
                    if k >= 1:
                        store(k - 1, (k - 1) % 4)
                    if k + 3 < NBLK:
                        load(k + 3, (k + 3) % 4)
                store(NBLK - 1, (NBLK - 1) % 4)
                for r in range(2):
                    sp.wait_ge(x3_stored[r], 16 * NBLK // 2)
                    sp.wait_ge(xt_stored[r], 16 * NBLK // 2)
                sp.wait_ge(w_loaded, 16 * 6)

            @blk.tensor
            def _(pe):
                def slot(q, m):
                    def center_x2():
                        on, t, r, s = stage(q, m, 0)
                        if on:
                            if s == 0:
                                pe.wait_ge(x2_loaded[r], 16 * (q + 1))
                            if past(t, 1):
                                pe.wait_ge(normed, t)
                            pe.matmul(pa3[:, :], center, xb[:, r, cols_of(s)], start=True,
                                      stop=True).then_inc(centered, 1)

                    def query():
                        on, t, r, s = stage(q, m, 1)
                        if on:
                            pe.wait_ge(normed, t + 1)
                            if past(t, 1):
                                pe.wait_ge(mapped, t)
                            pe.matmul(pq[:, :], qT[:, :], xn[:, s % 2, :], start=True, stop=True).then_inc(q_ready, 1)

                    def gate():
                        on, t, r, s = stage(q, m, 4)
                        if on:
                            pe.wait_ge(x3_ready, t + 1)
                            if past(t, 2):
                                pe.wait_ge(scaled, t - 1)
                            pe.matmul(px[s % 2][:, :], gateT[:, s % 2 * P:(s % 2 + 1) * P], x3[:, r % 2, cols_of(s)],
                                      start=True, stop=True).then_inc(projected, 1)

                    def moments():
                        on, t, r, s = stage(q, m, 4)
                        if on:
                            pair, _, _ = pair_of(q, m, 4)
                            pe.wait_ge(squared4, t + 1)
                            if s % 2 == 0 and past(t, 2):
                                pe.wait_ge(var4_ready, pair)
                            pe.matmul(pe2[:, :], (pair_mean[:, 64:64 + P], pair_mean[:, 0:P])[s % 2], sq4[:, s % 2, :],
                                      start=(s % 2 == 0), stop=(s % 2 == 1)).then_inc(moment_ready, 1)

                    def variance():
                        on, t, r, s = stage(q, m, 0)
                        if on:
                            pe.wait_ge(squared, t + 1)
                            if past(t, 1):
                                pe.wait_ge(ln_done, t)
                            pe.matmul(pv3[:, :], meanm, sq[:, :], start=True, stop=True).then_inc(var_ready, 1)

                    def denominator():
                        on, t, r, s = stage(q, m, 2)
                        if on:
                            pe.wait_ge(mapped, t + 1)
                            if past(t, 1):
                                pe.wait_ge(lnd_done, t)
                            pe.matmul(pd[:, :], dT[:, :], qm[:, s % 2, :], start=True, stop=True).then_inc(d_ready, 1)

                    def attend():
                        on, t, r, s = stage(q, m, 3)
                        if on:
                            pe.wait_ge(qz_ready, t + 1)
                            if past(t, 1):
                                pe.wait_ge(x3_ready, t)
                            pe.matmul(pm3[:, :], mT[:, :], qz[:, s % 2, :], start=True, stop=True).then_inc(m_ready, 1)

                    if m % 2:
                        center_x2(), gate(), query(), variance(), moments(), denominator(), attend()
                    else:
                        center_x2(), query(), variance(), denominator(), attend(), gate(), moments()
                schedule(pe, slot)

            @blk.scalar
            def _(act):
                act.preload_act_table_set("natural_log_exp_and_others")

                def slot(q, m):
                    def square_x2():
                        on, t, r, s = stage(q, m, 0)
                        if on:
                            act.wait_ge(centered, t + 1)
                            if past(t, 1):
                                act.wait_ge(var_ready, t)
                            act.activation(sq[:, :], pa3[:, :], ACT.Square).then_inc(squared, 1)

                    def square_x3():
                        on, t, r, s = stage(q, m, 4)
                        if on:
                            act.wait_ge(x3_ready, t + 1)
                            if past(t, 2):
                                act.wait_ge(moment_ready, t - 1)
                            act.activation(sq4[:, s % 2, :], x3[:, r % 2, cols_of(s)], ACT.Square).then_inc(squared4, 1)

                    def exp_query():
                        on, t, r, s = stage(q, m, 1)
                        if on:
                            act.wait_ge(q_ready, t + 1)
                            if past(t, 2):
                                act.wait_ge(mapped, t - 1)
                            act.activation(eq[:, s % 2, :], pq[:, :], ACT.Exp, bias=qb).then_inc(expq_ready, 1)

                    def square_mean():
                        on, t, r, s = stage(q, m, 4)
                        if on:
                            pair, ring, half = pair_of(q, m, 4)
                            act.wait_ge(projected, t + 1)
                            if past(pair, 2):
                                act.wait_ge(var4_ready, pair - 1)
                            act.activation(mean_sq[half, ring, :], px[s % 2][64 - half.start:P - half.start, :],
                                           ACT.Square).then_inc(mean_squared, 1)

                    def rstd_x2():
                        on, t, r, s = stage(q, m, 0)
                        if on:
                            act.wait_ge(var_ready, t + 1)
                            if past(t, 1):
                                act.wait_ge(rstd_ready, t)
                            act.activation(ln[:, 0, :], pv3[:, :], ACT.Ln, bias=eps_c).then_inc(ln_done, 1)
                            act.wait_ge(ln_done, t + 1)
                            if past(t, 2):
                                act.wait_ge(normed, t - 1)
                            act.activation(rstd[:, 0, s % 2, :], ln[:, 0, :], ACT.Exp, scale=-0.5).then_inc(rstd_ready, 1)

                    def inverse_denominator():
                        on, t, r, s = stage(q, m, 2)
                        if on:
                            act.wait_ge(d_ready, t + 1)
                            if past(t, 1):
                                act.wait_ge(z_ready, t)
                            act.activation(lnd[:, :], pd[:, :], ACT.Ln, bias=eps_z).then_inc(lnd_done, 1)
                            act.wait_ge(lnd_done, t + 1)
                            if past(t, 2):
                                act.wait_ge(qz_ready, t - 1)
                            act.activation(zr[:, s % 2, :], lnd[:, :], ACT.Exp, scale=-1.0).then_inc(z_ready, 1)

                    def exp_logits():
                        on, t, r, s = stage(q, m, 8)
                        if on and s == TPB - 1:
                            k = UNROLL * q + (m - 8) // TPB
                            act.wait_ge(neg_ready, k + 1)
                            if past(k, 2):
                                act.wait_ge(gathered, k - 1)
                            if past(k, 1):
                                act.wait_ge(expsum_ready, k)
                            act.activation(eg[:, :], lg[:, r % 2, :], ACT.Exp, bias=nm[:, r % 2, :],
                                           accum_out=se[:, r % 2, :]).then_inc(expsum_ready, 1)

                    def rstd_x3():
                        on, t, r, s = stage(q, m, 5)
                        if on and s % 2 == 1:
                            pair, ring, _ = pair_of(q, m, 5)
                            act.wait_ge(clamped, pair + 1)
                            if past(pair, 1):
                                act.wait_ge(rstd4_ready, pair)
                            act.activation(ln[:, 1, :], var4[:, :], ACT.Ln, bias=eps_t).then_inc(ln4_done, 1)
                            act.wait_ge(ln4_done, pair + 1)
                            if past(pair, 2):
                                act.wait_ge(scaled, 2 * pair - 2)
                            act.activation(rstd[:, 1, ring, :], ln[:, 1, :], ACT.Exp, scale=-0.5).then_inc(rstd4_ready, 1)

                    if m % 2:
                        square_x3(), square_x2(), square_mean(), exp_query(), rstd_x2(), exp_logits(), inverse_denominator()
                    else:
                        square_x2(), rstd_x3(), rstd_x2(), square_x3(), exp_query(), inverse_denominator(), square_mean()
                schedule(act, slot)

            @blk.gpsimd
            def _(pool):
                def pair_steps(k, r, pair):
                    g = 2 * k + pair
                    pool.wait_ge(scaled, 2 * g + 2)
                    at = lg[:, r, pair * TILE:(pair + 1) * TILE]
                    pool.tensor_tensor(at, at, gb.to_broadcast([P, TILE]), ALU.add).then_inc(biased, 1)

                def gather_best(k, r):
                    pool.wait_ge(at_ready, k + 1)
                    pool.wait_ge(expsum_ready, k + 1)
                    pool.sem_inc(held, 1)
                    pool.tensor_copy(cand[:, bass.ds(k * K, K)], m8[:, r, :])
                    pool.tensor_copy(cidx[:, bass.ds(k * K, K)], i8[:, r, :])
                    pool.tensor_copy(ses[:, bass.ds(k, 1)], se[:, r, :]).then_inc(gathered, 1)

                def block_steps(k, r, first=False):
                    pair_steps(k, r, 0)
                    if not first:
                        gather_best(k - 1, 1 - r)
                    pair_steps(k, r, 1)

                block_steps(0, 0, first=True)
                block_steps(1, 1)
                with pool.Fori(1, NBLK // 2) as two:
                    for r in range(2):
                        block_steps(2 * two + r, r)
                gather_best(NBLK - 1, (NBLK - 1) % 2)

            @blk.vector
            def _(dve):
                def slot(q, m):
                    def scale_logits():
                        on, t, r, s = stage(q, m, 5)
                        if on and s % 2 == 1:
                            pair, ring, _ = pair_of(q, m, 5)
                            k = UNROLL * q + (m - 5) // TPB
                            dve.wait_ge(rstd4_ready, pair + 1)
                            if s == 1 and past(k, 2):
                                dve.wait_ge(expsum_ready, k - 1)
                            for j in range(2):
                                half = slice(j * 64, (j + 1) * 64)
                                dve.tensor_tensor(lg[half, r % 2, s // 2 * TILE:(s // 2 + 1) * TILE], px[j][half, :],
                                                  rstd[half, 1, ring, :], ALU.mult).then_inc(scaled, 1)

                    def map_query():
                        on, t, r, s = stage(q, m, 1)
                        if on:
                            dve.wait_ge(expq_ready, t + 1)
                            dve.tensor_scalar(rq[:, s % 2, :], pq[:, :], qb, 0.0, ALU.add, ALU.max).then_inc(relu_ready, 1)
                            dve.wait_ge(relu_ready, t + 1)
                            if past(t, 2):
                                dve.wait_ge(d_ready, t - 1)
                            dve.scalar_tensor_tensor(out=qm[:, s % 2, :], in0=eq[:, s % 2, :], scalar=1.0,
                                                     in1=rq[:, s % 2, :], op0=ALU.min, op1=ALU.add).then_inc(mapped, 1)

                    def turn_x3():
                        on, t, r, s = stage(q, m, 4)
                        if on:
                            k = UNROLL * q + (m - 4) // TPB
                            dve.wait_ge(x3_ready, t + 1)
                            if s == 0 and past(k, 2):
                                dve.wait_ge(xt_stored[r % 2], 16 * (2 * q + (m - 4) // (2 * TPB)))
                            dve.transpose(xt[:, r % 2, cols_of(s)], x3[:, r % 2, cols_of(s)]).then_inc(turned, 1)

                    def variance_x3():
                        on, t, r, s = stage(q, m, 4)
                        if on and s % 2 == 1:
                            pair, ring, _ = pair_of(q, m, 4)
                            dve.wait_ge(moment_ready, t + 1)
                            dve.wait_ge(mean_squared, t + 1)
                            if past(pair, 1):
                                dve.wait_ge(ln4_done, pair)
                            dve.tensor_tensor(var4[:, :], pe2[:, :], mean_sq[:, ring, :], ALU.subtract).then_inc(var4_ready, 1)
                            dve.wait_ge(var4_ready, pair + 1)
                            dve.tensor_scalar(var4[:, :], var4[:, :], 0.0, None, ALU.max).then_inc(clamped, 1)

                    def norm_x2():
                        on, t, r, s = stage(q, m, 0)
                        if on:
                            dve.wait_ge(rstd_ready, t + 1)
                            if past(t, 2):
                                dve.wait_ge(q_ready, t - 1)
                            dve.tensor_tensor(xn[:, s % 2, :], pa3[:, :], rstd[:, 0, s % 2, :], ALU.mult).then_inc(normed, 1)

                    def query_by_inverse():
                        on, t, r, s = stage(q, m, 2)
                        if on:
                            dve.wait_ge(mapped, t + 1)
                            dve.wait_ge(z_ready, t + 1)
                            if past(t, 2):
                                dve.wait_ge(m_ready, t - 1)
                            dve.tensor_tensor(qz[:, s % 2, :], qm[:, s % 2, :], zr[:, s % 2, :], ALU.mult).then_inc(qz_ready, 1)

                    def best_logits():
                        on, t, r, s = stage(q, m, 6)
                        if on and s == TPB - 1:
                            k = UNROLL * q + (m - 6) // TPB
                            dve.wait_ge(biased, 2 * k + 2)
                            if past(k, 2):
                                dve.wait_ge(gathered, k - 1)
                            dve.sem_inc(held, 1)
                            dve.max(m8[:, r % 2, :], lg[:, r % 2, :]).then_inc(best_ready, 1)

                    def best_logits_at():
                        on, t, r, s = stage(q, m, 6)
                        if on and s == TPB - 1:
                            k = UNROLL * q + (m - 6) // TPB
                            dve.wait_ge(best_ready, k + 1)
                            dve.sem_inc(held, 1)
                            dve.max_index(i8[:, r % 2, :], m8[:, r % 2, :], lg[:, r % 2, :]).then_inc(at_ready, 1)
                            dve.tensor_scalar(nm[:, r % 2, :], m8[:, r % 2, 0:1], -1.0, None, ALU.mult).then_inc(neg_ready, 1)

                    def add_attention():
                        on, t, r, s = stage(q, m, 3)
                        if on:
                            dve.wait_ge(m_ready, t + 1)
                            k = UNROLL * q + (m - 3) // TPB
                            if s == 0 and past(k, 2):
                                dve.wait_ge(projected, 4 * k - 4)
                                dve.wait_ge(squared4, 4 * k - 4)
                                dve.wait_ge(turned, 4 * k - 4)
                                dve.wait_ge(x3_stored[r % 2], 16 * (2 * q + (m - 3) // (2 * TPB)))
                            dve.scalar_tensor_tensor(out=x3[:, r % 2, cols_of(s)], in0=pm3[:, :], scalar=pb,
                                                     in1=xb[:, r, cols_of(s)], op0=ALU.add, op1=ALU.add).then_inc(x3_ready, 1)

                    if m % 2:
                        turn_x3(), best_logits(), map_query(), norm_x2(), variance_x3(), best_logits_at()
                        query_by_inverse(), add_attention()
                    else:
                        scale_logits(), turn_x3(), norm_x2(), add_attention(), map_query(), query_by_inverse()
                schedule(dve, slot)

        with ExitStack() as ph:
            NC = NBLK * K
            c2 = sb("c2", [64, 2 * NC], F32, ph)
            i2 = sb("i2", [64, 2 * NC], F32, ph)
            se2 = sb("se2", [64, 2 * NBLK], F32, ph)
            ex = sb("ex", [64, 2 * NBLK], F32, ph)
            jk = sb("jk", [64, 2 * NC], F32, ph)
            t8 = sb("t8", [64, K], F32, ph)
            a8 = sb("a8", [64, K], U32, ph)
            a8f = sb("a8f", [64, K], F32, ph)
            nmx = sb("nmx", [64, 4], F32, ph)
            tokf = sb("tokf", [64, K], F32, ph)
            toki = sb("toki", [64, K], I32, ph)
            prob = sb("prob", [64, K], F32, ph)
            half = sb("half_of_pair", [P, NC], F32, ph)
            toki2 = sb("token_of_slot", [P, B, 2], I32, ph)
            row_terms = sb("row_terms", [P, 3, B, 2], I32, ph)
            row0 = sb("row_of_slot", [P, B, 2], I32, ph)
            row_at = sb("row_at", [P, 2, B, 2], I32, ph)
            xs = sb("x3_of_slot", [P, 2, P], F32, ph)
            eq_later = sb("eq_later", [P, B, 2, E * K], F32, ph)
            wide_ones = sb("wide_ones", [P, C], F32, ph)
            tokq = sb("token_by_channel", [P, E * K], F32, ph)
            repeat = sb("repeat", [P, E * K], F32, ph)
            word = sb("word_of_slot", [P, E * K], I32, ph)
            toki_b = sb("token_of_batch", [P, E * K], I32, ph)
            repeat_b = sb("repeat_of_batch", [P, E * K], I32, ph)
            NS = E * K
            tokr = sb("tokr", [P, B, NS], F32, ph)
            tokc = sb("tokc", [P, B, 2], F32, ph)
            pr = sb("pr", [P, NS], F32, ph)
            xg = sb("xg", [P, NS], F32, ph)
            sqg = sb("sqg", [P, NS], F32, ph)
            lng = sb("lng", [P, NS], F32, ph)
            xgn = sb("xgn", [P, NS], F32, ph)
            pool_sb = sb("pool_sb", [P, E], F32, ph)
            hin = sb("hin", [P, E // 2, 2, B], F32, ph)
            h1 = sb("h1", [P, 2, E, B], F32, ph)
            o_sb = sb("o_sb", [C, E, B], F32, ph)
            wv = sb("wv", [P, NS], F32, ph)
            wvT = sb("wvT", [P, 2, P], F32, ph)
            eqm = sb("eqm", [P, B, 2, NS], F32, ph)
            fin = sb("fin", [P, NS], F32, ph)
            pgn = ph.enter_context(nc.psum_tensor("pgn", [P, NS], F32))
            pgv = ph.enter_context(nc.psum_tensor("pgv", [P, NS], F32))
            php = ph.enter_context(nc.psum_tensor("php", [C, B, E], F32))
            pgx, prep = pgv, pgn
            ph1 = ph.enter_context(nc.psum_tensor("ph1", [P, 2, E, B], F32))
            po = ph.enter_context(nc.psum_tensor("po", [C, E, B], F32))
            po2 = ph.enter_context(nc.psum_tensor("po2", [P, E], F32))
            pt = ph.enter_context(nc.psum_tensor("pt", [P, 2, P], F32))
            pc = ph.enter_context(nc.psum_tensor("pc", [P, NS], F32))
            S = lambda n: sem(n, ph)
            placed, merged, out_tok, back, dv, ac, mm, gath, scat = (
                S(n) for n in ("placed", "merged", "tokens_out", "tokens_back", "tail_vector", "tail_scalar", "tail_tensor", "columns_in", "columns_out"))
            gp = S("tail_pool")
            scat0, scat1 = S("columns_out_batch0"), S("columns_out_batch1")
            back2, rep, turned_back = S("broadcasts_back"), S("repeats_counted"), S("tokens_turned")
            blk = ph.enter_context(nc.Block())
            ONE = dict(allow_slow_non_contiguous=True)

            SHARED = 76
            SKIP = float(2 ** 28)
            out_words = out.rearrange("b c h w -> (b c h w)").rearrange("(n o) -> n o", o=1)
            xt_rows = xt_d.rearrange("k p (m j) -> (k p m) j", j=32)

            def scatter(eng, b, signal):
                rows = slice(b * C, (b + 1) * C)
                with eng.Fori(0, SHARED // 4) as i:
                    for v in range(4):
                        s = i * 4 + (NS - SHARED + v)
                        tok = eng.value_load(toki_b[b * C:b * C + 1, bass.ds(s, 1)], min_val=0, max_val=N - 1)
                        more = eng.value_load(repeat_b[b * C:b * C + 1, bass.ds(s, 1)], min_val=0, max_val=1)
                        with eng.If(more == 0):
                            eng.dma_start(out_v[rows, bass.ds(tok, 1)], fin[rows, bass.ds(s, 1)], **ONE).then_inc(signal, 16)
                        with eng.Else():
                            eng.sem_inc(signal, 16)
                eng.wait_ge(signal, 16 * SHARED)

            @blk.sync
            def _(sp):
                sp.wait_ge(placed, 1)
                for j in range(2):
                    rows = slice(j * 64, (j + 1) * 64)
                    sp.dma_start(c2[:, j * NC:(j + 1) * NC], cand[rows, :]).then_inc(merged, 16)
                    sp.dma_start(i2[:, j * NC:(j + 1) * NC], cidx[rows, :]).then_inc(merged, 16)
                    sp.dma_start(se2[:, j * NBLK:(j + 1) * NBLK], ses[rows, :]).then_inc(merged, 16)
                sp.wait_ge(dv, DV_TOK)
                sp.dma_start(tok_d.rearrange("(p k) -> p k", k=K), toki[:, :]).then_inc(out_tok, 16)
                sp.dma_start(tokf_d.rearrange("(p k) -> p k", k=K), tokf[:, :]).then_inc(out_tok, 16)
                sp.dma_start(prob_d.rearrange("(p k) -> p k", k=K), prob[:, :]).then_inc(out_tok, 16)
                sp.wait_ge(out_tok, 48)
                sp.dma_start(toki2[:, :, :].rearrange("p b j -> p (b j)"), tok_d.rearrange("(n p) -> p n", p=P), **ONE).then_inc(back, 16)
                sp.dma_start(tokc[:, :, :].rearrange("p b j -> p (b j)"), tokf_d.rearrange("(n p) -> p n", p=P), **ONE).then_inc(back2, 16)
                for b in range(B):
                    rows = slice(b * C, (b + 1) * C)
                    sp.dma_start(tokr[:, b, :], tokf_d[b * NS:(b + 1) * NS].partition_broadcast(P)).then_inc(back2, 16)
                    sp.dma_start(tokq[rows, :], tokf_d[b * NS:(b + 1) * NS].partition_broadcast(C)).then_inc(back2, 16)
                    sp.dma_start(pr[rows, :], prob_d[b * NS:(b + 1) * NS].partition_broadcast(C)).then_inc(back2, 16)
                sp.wait_ge(back2, 16 * 7)
                sp.wait_ge(dv, DV_FIN)
                scatter(sp, 0, scat0)

            @blk.scalar
            def _(act):
                act.preload_act_table_set("natural_log_exp_and_others")
                act.wait_ge(dv, DV_MAX)
                act.activation(ex[:, :], c2[:, ::K], ACT.Exp, bias=nmx[:, 0:1]).then_inc(ac, 1)
                act.activation(prob[:, :], t8[:, :], ACT.Exp, bias=nmx[:, 0:1]).then_inc(ac, 1)
                act.wait_ge(mm, 1)
                act.activation(sqg[:, :], pgn[:, :], ACT.Square).then_inc(ac, 1)
                act.wait_ge(mm, 2)
                act.activation(lng[:, :], pgv[:, :], ACT.Ln, bias=eps_t).then_inc(ac, 1)
                act.wait_ge(ac, 4)
                act.activation(lng[:, :], lng[:, :], ACT.Exp, scale=-0.5).then_inc(ac, 1)
                act.preload_act_table(ACT.Gelu)
                act.wait_ge(mm, 4)
                act.activation(h1[:, :, :, :].rearrange("p j e b -> p (j e b)"),
                               ph1[:, :, :, :].rearrange("p j e b -> p (j e b)"), ACT.Gelu).then_inc(ac, 1)
                act.wait_ge(dv, DV_FIN)
                scatter(act, 1, scat1)

            @blk.gpsimd
            def _(pool):
                pool.memset(hin[:, :, :, :], 0.0).then_inc(gp, 1)
                pool.wait_ge(gp, 1)
                pool.memset(wide_ones[:, :], 1.0).then_inc(gp, 1)
                pool.wait_ge(dv, DV_ROWS)
                for h in range(2):
                    for b in range(B):
                        for j in range(2):
                            pool.indirect_dma_start(
                                out=xs[:, j, b * C + h * 32:b * C + h * 32 + 32], out_offset=None, in_=xt_rows,
                                in_offset=bass.IndirectOffsetOnAxis(ap=row_at[:, h, b, j:j + 1], axis=0)).then_inc(gath, 16)
                pool.wait_ge(dv, DV_FIN)
                for s in range(NS - SHARED):
                    pool.indirect_dma_start(
                        out=out_words, out_offset=bass.IndirectOffsetOnAxis(ap=word[:, s:s + 1], axis=0),
                        in_=fin[:, s:s + 1], in_offset=None, bounds_check=B * C * N - 1,
                        oob_is_err=False).then_inc(scat, 16)
                pool.wait_ge(scat, 16 * (NS - SHARED))

            n_dv = [0]

            @blk.tensor
            def _(pe):
                pe.wait_ge(gp, 2)
                pe.wait_ge(dv, DV_EQ)
                for b in range(B):
                    for j in range(2):
                        m = pe.matmul(prep[b * C:(b + 1) * C, :], wide_ones[:, :], eq_later[:, b, j, :],
                                      start=(j == 0), stop=(j == 1))
                m.then_inc(rep, 1)
                pe.wait_ge(gath, 16 * 8)
                for j in range(2):
                    m = pe.transpose(pgx[:, j * P:(j + 1) * P], xs[:, j, :], ident)
                m.then_inc(turned_back, 1)
                pe.wait_ge(dv, DV_XG)
                pe.matmul(pgn[:, :], center, xg[:, :], start=True, stop=True).then_inc(mm, 1)
                pe.wait_ge(ac, 3)
                pe.matmul(pgv[:, :], meanm, sqg[:, :], start=True, stop=True).then_inc(mm, 1)
                pe.wait_ge(dv, DV_POOL)
                for b in range(B):
                    m = pe.matmul(php[:, b, :], ident[:, b * C:(b + 1) * C], pool_sb[:, :], start=True, stop=True)
                m.then_inc(mm, 1)
                pe.wait_ge(dv, DV_HIN)
                pe.wait_ge(gp, 1)
                each_twice = ident[0:E, 0:E].unsqueeze(2).to_broadcast([E, E, B])
                for j in range(2):
                    pe.matmul(ph1[:, j, :, :], w1b_sb[:, j * P:(j + 1) * P], each_twice, start=True,
                              stop=False, skip_group_check=True)
                    for i in range(E // 2):
                        m = pe.matmul(ph1[:, j, 2 * i:2 * i + 2, :], w1_sb[:, i, j * P:(j + 1) * P], hin[:, i, :, :],
                                      start=False, stop=True, skip_group_check=True)
                m.then_inc(mm, 1)
                pe.wait_ge(ac, 6)
                pe.matmul(po[:, :, :], w2b_sb[:, :], each_twice, start=True,
                          stop=False, skip_group_check=True)
                for e in range(E):
                    for j in range(2):
                        m = pe.matmul(po[:, e, :], w2_sb[:, j, e, :], h1[:, j, e, :], start=False,
                                      stop=(j == 1), skip_group_check=True)
                m.then_inc(mm, 1)
                pe.wait_ge(dv, DV_OUT)
                for b in range(B):
                    m = pe.matmul(po2[b * C:(b + 1) * C, :], ident[0:C, 0:C], o_sb[:, :, b], start=True, stop=True)
                m.then_inc(mm, 1)
                pe.wait_ge(dv, DV_WV)
                for j in range(2):
                    m = pe.transpose(pt[:, j, :], wv[:, j * P:(j + 1) * P], ident)
                m.then_inc(mm, 1)
                pe.wait_ge(dv, DV_WVT)
                for b in range(B):
                    for j in range(2):
                        m = pe.matmul(pc[b * C:(b + 1) * C, :], wvT[:, j, b * C:(b + 1) * C], eqm[:, b, j, :],
                                      start=(j == 0), stop=(j == 1))
                m.then_inc(mm, 1)

            @blk.vector
            def _(dve):
                did = n_dv

                def go(ins):
                    did[0] += 1
                    ins.then_inc(dv, 1)
                    dve.wait_ge(dv, did[0])

                go(dve.tensor_scalar(half[:, :], cidx[:, :], float(TILE), float(TILE), ALU.is_ge, ALU.mult))
                go(dve.tensor_tensor(half[:, :], half[:, :], base_c, ALU.add))
                dve.tensor_tensor(cidx[:, :], cidx[:, :], half[:, :], ALU.add).then_inc(placed, 1)
                dve.wait_ge(merged, 96)
                go(dve.max(t8[:, :], c2[:, :]))
                go(dve.tensor_scalar(nmx[:, 0:1], t8[:, 0:1], -1.0, None, ALU.mult))
                assert did[0] == DV_MAX
                go(dve.max_index(a8[:, :], t8[:, :], c2[:, :]))
                go(dve.tensor_copy(a8f[:, :], a8[:, :]))
                for k in range(K):
                    go(dve.scalar_tensor_tensor(out=jk[:, :], in0=iota_c[0:64, :], scalar=a8f[:, k:k + 1],
                                                in1=i2[:, :], op0=ALU.is_equal, op1=ALU.mult,
                                                accum_out=tokf[:, k:k + 1]))
                go(dve.tensor_copy(toki[:, :], tokf[:, :]))
                dve.wait_ge(ac, 2)
                go(dve.scalar_tensor_tensor(out=jk[:, 0:2 * NBLK], in0=ex[:, :], scalar=1.0, in1=se2[:, :],
                                            op0=ALU.mult, op1=ALU.mult, accum_out=nmx[:, 1:2]))
                go(dve.reciprocal(nmx[:, 2:3], nmx[:, 1:2]))
                go(dve.tensor_scalar(prob[:, :], prob[:, :], nmx[:, 2:3], None, ALU.mult))
                assert did[0] == DV_TOK
                dve.wait_ge(back, 16)
                for i, (op0, n0, op1, n1) in enumerate((
                        (ALU.logical_shift_right, 11, ALU.logical_shift_left, 13),
                        (ALU.bitwise_and, 31, ALU.logical_shift_left, 6),
                        (ALU.logical_shift_right, 5, ALU.bitwise_and, 63))):
                    go(dve.tensor_scalar(row_terms[:, i, :, :], toki2[:, :, :], n0, n1, op0, op1))
                go(dve.tensor_tensor(row0[:, :, :], row_terms[:, 0, :, :], row_terms[:, 1, :, :], ALU.add))
                go(dve.tensor_tensor(row0[:, :, :], row0[:, :, :], row_terms[:, 2, :, :], ALU.add))
                for h in range(2):
                    for b in range(B):
                        go(dve.tensor_scalar(row_at[:, h, b, :], row0[:, b, :], float((2 * b + h) * BLOCK), None, ALU.add))
                assert did[0] == DV_ROWS
                dve.wait_ge(back2, 16 * 7)
                for b in range(B):
                    for j in range(2):
                        go(dve.tensor_scalar(eqm[:, b, j, :], tokr[:, b, :], tokc[:, b, j:j + 1], None, ALU.is_equal))
                        go(dve.tensor_tensor(eq_later[:, b, j, :], eqm[:, b, j, :], later[:, j, :], ALU.mult))
                assert did[0] == DV_EQ
                dve.wait_ge(rep, 1)
                go(dve.tensor_scalar(repeat[:, :], prep[:, :], 0.0, SKIP, ALU.is_gt, ALU.mult))
                go(dve.scalar_tensor_tensor(out=word[:, :], in0=tokq[:, :], scalar=start_c, in1=repeat[:, :],
                                            op0=ALU.add, op1=ALU.add))
                go(dve.tensor_copy(toki_b[:, :], tokq[:, :]))
                go(dve.tensor_scalar(repeat_b[:, :], prep[:, :], 0.0, None, ALU.is_gt))
                dve.wait_ge(turned_back, 1)
                go(dve.tensor_copy(xg[:, :], pgx[:, :]))
                assert did[0] == DV_XG
                dve.wait_ge(ac, 5)
                go(dve.tensor_tensor(xgn[:, :], pgn[:, :], lng[:, :], ALU.mult))
                go(dve.tensor_tensor(xgn[:, :], xgn[:, :], pr[:, :], ALU.mult))
                go(dve.tensor_reduce(pool_sb[:, :], xgn[:, :].rearrange("p (e k) -> p e k", k=K), AX.X, ALU.add))
                assert did[0] == DV_POOL
                dve.wait_ge(mm, 3)
                dve.wait_ge(gp, 1)
                for j in range(2):
                    go(dve.tensor_copy(hin[j * C:(j + 1) * C, :, j, :], php[:, :, j::2].rearrange("c b i -> c i b")))
                assert did[0] == DV_HIN
                dve.wait_ge(mm, 5)
                go(dve.tensor_copy(o_sb[:, :, :], po[:, :, :]))
                assert did[0] == DV_OUT
                dve.wait_ge(mm, 6)
                go(dve.tensor_tensor(wv[:, :].rearrange("p (e k) -> p e k", k=K),
                                     pr[:, :].rearrange("p (e k) -> p e k", k=K),
                                     po2[:, :].unsqueeze(2).to_broadcast([P, E, K]), ALU.mult))
                assert did[0] == DV_WV
                dve.wait_ge(mm, 7)
                go(dve.tensor_copy(wvT[:, :, :], pt[:, :, :]))
                assert did[0] == DV_WVT
                dve.wait_ge(mm, 8)
                go(dve.tensor_tensor(fin[:, :], xg[:, :], pc[:, :], ALU.add))
                assert did[0] == DV_FIN


DV_MAX = 4
DV_TOK = DV_MAX + 2 + K + 1 + 3
DV_ROWS = DV_TOK + 3 + 2 + 4
DV_EQ = DV_ROWS + 2 * 4
DV_XG = DV_EQ + 4 + 1
DV_POOL = DV_XG + 3
DV_HIN = DV_POOL + 2
DV_OUT = DV_HIN + 1
DV_WV = DV_OUT + 1
DV_WVT = DV_WV + 1
DV_FIN = DV_WVT + 1

_INS = ["x", "L0_conv_kernel", "L0_ffn_W", "L0_ffn_V", "L0_ffn_gamma", "L0_ffn_beta", "L1_conv_q_w",
        "L1_conv_q_b", "L1_conv_kv_w", "L1_conv_kv_b", "L1_conv_proj_w", "L1_conv_proj_b",
        "L1_ffn_gate_w", "L1_ffn_gate_b", "L1_ffn_weight1", "L1_ffn_weight2"]


def kernel(**inputs):
    import concourse.bacc as bacc
    from concourse.bass_utils import run_bass_kernel_spmd

    nc = bacc.Bacc("TRN2", target_bir_lowering=False, num_devices=1)
    arrays, args = {}, []
    for name, a in [(n, inputs[n]) for n in _INS] + [("constants", constants())]:
        a = np.ascontiguousarray(a)
        arrays[f"in_{name}"] = a
        args.append(nc.dram_tensor(f"in_{name}", a.shape, mybir.dt.from_np(a.dtype), kind="ExternalInput").ap())
    args.append(nc.dram_tensor("out_0", (B, C, H, W), F32, kind="ExternalOutput").ap())
    build_program(nc, *args)
    r = run_bass_kernel_spmd(nc, [arrays], core_ids=[0])
    return r.results[0]["out_0"]
```
